# Optimizing a Trainium2 kernel written in Bass

```python
import numpy as np
import jax
import jax.numpy as jnp

def _softmax(x, axis=-1):
    return jax.nn.softmax(x, axis=axis)
def _gelu(x):
    return jax.nn.gelu(x, approximate=True)
def _silu(x):
    return jax.nn.silu(x)
def _sigmoid(x):
    return jax.nn.sigmoid(x)
def _layernorm(x, axis=-1, eps=1e-5):
    m = jnp.mean(x, axis=axis, keepdims=True)
    v = jnp.var(x, axis=axis, keepdims=True)
    return (x - m) / jnp.sqrt(v + eps)
def _scatter_add(tgt, idx, src, axis=0):
    return tgt.at[idx].add(src)
def _segment_sum(src, seg, n):
    return jax.ops.segment_sum(src, seg, n)

kernel_name = 'mk_conv_seq_d2_conv_nhwc64_0f0246'

def setup_inputs(seed: int = 0):
    np.random.seed(seed)
    _w = jnp.asarray
    def _rec_inputs():
        import jax
        import jax.numpy as jnp
        _gk = jax.random.key(seed)
        x = -0.000125 + 0.9999 * jax.random.normal(jax.random.fold_in(_gk, 1), (8, 256, 256, 64), jnp.float32)
        return x
    x = _rec_inputs()
    def _L0_conv_setup():
        import jax, jax.numpy as jnp
        import numpy as np
        import math
        DIM = 64
        NUM_HEADS = 4
        HEAD_DIM = DIM // NUM_HEADS
        WS = (4, 4)
        SS = (8, 8)

        def _rel_position_index():
            ch, cw = np.meshgrid(np.arange(WS[0]), np.arange(WS[1]), indexing='ij')
            coords = np.stack([ch, cw]).reshape(2, -1)
            rel = (coords[:, :, None] - coords[:, None, :]).transpose(1, 2, 0)
            rel[:, :, 0] += WS[0] - 1
            rel[:, :, 1] += WS[1] - 1
            rel[:, :, 0] *= 2 * WS[1] - 1
            return rel.sum(-1).reshape(-1)

        def _rel_coords_table():
            h = np.arange(-(WS[0] - 1), WS[0], dtype=np.float32)
            w = np.arange(-(WS[1] - 1), WS[1], dtype=np.float32)
            t = np.stack(np.meshgrid(h, w, indexing='ij'), axis=-1)
            t[..., 0] /= WS[0] - 1
            t[..., 1] /= WS[1] - 1
            t *= 8.0
            t = np.sign(t) * np.log2(np.abs(t) + 1.0) / 3.0
            return t.reshape(-1, 2).astype(np.float32)

        def _attn_mask(H, W):
            m = np.zeros((H, W), np.float32)
            hs = (slice(0, -WS[0]), slice(-WS[0], -SS[0]), slice(-SS[0], None))
            ws_ = (slice(0, -WS[1]), slice(-WS[1], -SS[1]), slice(-SS[1], None))
            cnt = 0
            for h in hs:
                for w in ws_:
                    m[h, w] = cnt
                    cnt += 1
            nWh, nWw = (H // WS[0], W // WS[1])
            m = m.reshape(nWh, WS[0], nWw, WS[1]).transpose(0, 2, 1, 3).reshape(nWh * nWw, WS[0] * WS[1])
            d = m[:, None, :] - m[:, :, None]
            return np.where(d != 0, -100.0, 0.0).astype(np.float32)

        def _layernorm(x, g, b):
            m = x.mean(-1, keepdims=True)
            v = x.var(-1, keepdims=True)
            return (x - m) / jnp.sqrt(v + 1e-05) * g + b

        def _shifted_window_attention(x, qkv_w, qkv_b, proj_w, proj_b, logit_scale, cpb_w1, cpb_b1, cpb_w2):
            B, H, W, C = x.shape
            nWh, nWw = (H // WS[0], W // WS[1])
            nW, N = (nWh * nWw, WS[0] * WS[1])
            xs = jnp.roll(x, (-SS[0], -SS[1]), axis=(1, 2))
            xw = xs.reshape(B, nWh, WS[0], nWw, WS[1], C).transpose(0, 1, 3, 2, 4, 5).reshape(B * nW, N, C)
            qkv_b = qkv_b.at[C:2 * C].set(0.0)
            qkv = xw @ qkv_w.T + qkv_b
            qkv = qkv.reshape(B * nW, N, 3, NUM_HEADS, HEAD_DIM).transpose(2, 0, 3, 1, 4)
            q, k, v = (qkv[0], qkv[1], qkv[2])
            qn = q / jnp.maximum(jnp.linalg.norm(q, axis=-1, keepdims=True), 1e-12)
            kn = k / jnp.maximum(jnp.linalg.norm(k, axis=-1, keepdims=True), 1e-12)
            attn = jnp.einsum('whnd,whmd->whnm', qn, kn)
            scale = jnp.exp(jnp.minimum(logit_scale, math.log(100.0)))
            attn = attn * scale[None]
            table = jax.nn.relu(jnp.asarray(_rel_coords_table()) @ cpb_w1.T + cpb_b1) @ cpb_w2.T
            bias = table[jnp.asarray(_rel_position_index())].reshape(N, N, NUM_HEADS).transpose(2, 0, 1)
            bias = 16.0 * jax.nn.sigmoid(bias)
            attn = attn + bias[None]
            mask = jnp.asarray(_attn_mask(H, W))
            attn = attn.reshape(B, nW, NUM_HEADS, N, N) + mask[None, :, None]
            attn = jax.nn.softmax(attn.reshape(B * nW, NUM_HEADS, N, N), axis=-1)
            out = jnp.einsum('whnm,whmd->whnd', attn, v).transpose(0, 2, 1, 3).reshape(B * nW, N, C)
            out = out @ proj_w.T + proj_b
            out = out.reshape(B, nWh, nWw, WS[0], WS[1], C).transpose(0, 1, 3, 2, 4, 5).reshape(B, H, W, C)
            return jnp.roll(out, (SS[0], SS[1]), axis=(1, 2))
        key = jax.random.key(seed)
        ks = jax.random.split(key, 16)
        B, H, W, C = (8, 256, 256, DIM)
        s = 0.02
        return {'x': jax.random.normal(ks[0], (B, H, W, C), jnp.float32), 'qkv_w': jax.random.normal(ks[1], (3 * C, C), jnp.float32) * s, 'qkv_b': jnp.zeros((3 * C,), jnp.float32), 'proj_w': jax.random.normal(ks[2], (C, C), jnp.float32) * s, 'proj_b': jnp.zeros((C,), jnp.float32), 'logit_scale': jnp.full((NUM_HEADS, 1, 1), math.log(10.0), jnp.float32), 'cpb_w1': jax.random.normal(ks[3], (512, 2), jnp.float32) * s, 'cpb_b1': jnp.zeros((512,), jnp.float32), 'cpb_w2': jax.random.normal(ks[4], (NUM_HEADS, 512), jnp.float32) * s, 'norm1_g': jnp.ones((C,), jnp.float32), 'norm1_b': jnp.zeros((C,), jnp.float32), 'norm2_g': jnp.ones((C,), jnp.float32), 'norm2_b': jnp.zeros((C,), jnp.float32), 'fc1_w': jax.random.normal(ks[5], (4 * C, C), jnp.float32) * s, 'fc1_b': jnp.zeros((4 * C,), jnp.float32), 'fc2_w': jax.random.normal(ks[6], (C, 4 * C), jnp.float32) * s, 'fc2_b': jnp.zeros((C,), jnp.float32)}
    _L0_conv_all = _L0_conv_setup()
    _L0_conv_in = {k: v for k, v in _L0_conv_all.items() if k in ('qkv_w', 'qkv_b', 'proj_w', 'proj_b', 'logit_scale', 'cpb_w1', 'cpb_b1', 'cpb_w2', 'norm1_g', 'norm1_b', 'norm2_g', 'norm2_b', 'fc1_w', 'fc1_b', 'fc2_w', 'fc2_b', )}
    del _L0_conv_all

    def _L1_conv_setup():
        import jax, jax.numpy as jnp
        import numpy as np
        KERNEL = 25
        NUM_MODES = 128

        def _moving_average(x, k):
            if k <= 1:
                return x
            left = k - 1 - (k - 1) // 2
            right = (k - 1) // 2
            xpad = jnp.concatenate([jnp.broadcast_to(x[:, :1], (x.shape[0], left) + x.shape[2:]), x, jnp.broadcast_to(x[:, -1:], (x.shape[0], right) + x.shape[2:])], axis=1)
            c = jnp.cumsum(xpad, axis=1)
            c = jnp.concatenate([jnp.zeros_like(c[:, :1]), c], axis=1)
            return (c[:, k:] - c[:, :-k]) / k
        key = jax.random.key(seed)
        k1, k2, k3 = jax.random.split(key, 3)
        B, T, N, C, M = (8, 512, 128, 64, NUM_MODES)
        x = jax.random.normal(k1, (B, T, N, C), dtype=jnp.float32)
        bound = float(np.sqrt(6.0 / (M + M)))
        w_real = jax.random.uniform(k2, (C, M, M), jnp.float32, -bound, bound)
        w_imag = jax.random.uniform(k3, (C, M, M), jnp.float32, -bound, bound)
        return {'x': x, 'w_real': w_real, 'w_imag': w_imag}
    _L1_conv_all = _L1_conv_setup()
    _L1_conv_in = {k: v for k, v in _L1_conv_all.items() if k in ('w_real', 'w_imag', )}
    del _L1_conv_all

    return {
        "x": x,
        "L0_conv_qkv_w": _L0_conv_in["qkv_w"],
        "L0_conv_qkv_b": _L0_conv_in["qkv_b"],
        "L0_conv_proj_w": _L0_conv_in["proj_w"],
        "L0_conv_proj_b": _L0_conv_in["proj_b"],
        "L0_conv_logit_scale": _L0_conv_in["logit_scale"],
        "L0_conv_cpb_w1": _L0_conv_in["cpb_w1"],
        "L0_conv_cpb_b1": _L0_conv_in["cpb_b1"],
        "L0_conv_cpb_w2": _L0_conv_in["cpb_w2"],
        "L0_conv_norm1_g": _L0_conv_in["norm1_g"],
        "L0_conv_norm1_b": _L0_conv_in["norm1_b"],
        "L0_conv_norm2_g": _L0_conv_in["norm2_g"],
        "L0_conv_norm2_b": _L0_conv_in["norm2_b"],
        "L0_conv_fc1_w": _L0_conv_in["fc1_w"],
        "L0_conv_fc1_b": _L0_conv_in["fc1_b"],
        "L0_conv_fc2_w": _L0_conv_in["fc2_w"],
        "L0_conv_fc2_b": _L0_conv_in["fc2_b"],
        "L1_conv_w_real": _L1_conv_in["w_real"],
        "L1_conv_w_imag": _L1_conv_in["w_imag"],
    }

def reference(x, L0_conv_qkv_w, L0_conv_qkv_b, L0_conv_proj_w, L0_conv_proj_b, L0_conv_logit_scale, L0_conv_cpb_w1, L0_conv_cpb_b1, L0_conv_cpb_w2, L0_conv_norm1_g, L0_conv_norm1_b, L0_conv_norm2_g, L0_conv_norm2_b, L0_conv_fc1_w, L0_conv_fc1_b, L0_conv_fc2_w, L0_conv_fc2_b, L1_conv_w_real, L1_conv_w_imag):
    import jax
    import jax.numpy as jnp
    def _L0_conv_ref(x, qkv_w, qkv_b, proj_w, proj_b, logit_scale, cpb_w1, cpb_b1, cpb_w2, norm1_g, norm1_b, norm2_g, norm2_b, fc1_w, fc1_b, fc2_w, fc2_b):
        import jax, jax.numpy as jnp
        import numpy as np
        import math
        DIM = 64
        NUM_HEADS = 4
        HEAD_DIM = DIM // NUM_HEADS
        WS = (4, 4)
        SS = (8, 8)

        def _rel_position_index():
            ch, cw = np.meshgrid(np.arange(WS[0]), np.arange(WS[1]), indexing='ij')
            coords = np.stack([ch, cw]).reshape(2, -1)
            rel = (coords[:, :, None] - coords[:, None, :]).transpose(1, 2, 0)
            rel[:, :, 0] += WS[0] - 1
            rel[:, :, 1] += WS[1] - 1
            rel[:, :, 0] *= 2 * WS[1] - 1
            return rel.sum(-1).reshape(-1)

        def _rel_coords_table():
            h = np.arange(-(WS[0] - 1), WS[0], dtype=np.float32)
            w = np.arange(-(WS[1] - 1), WS[1], dtype=np.float32)
            t = np.stack(np.meshgrid(h, w, indexing='ij'), axis=-1)
            t[..., 0] /= WS[0] - 1
            t[..., 1] /= WS[1] - 1
            t *= 8.0
            t = np.sign(t) * np.log2(np.abs(t) + 1.0) / 3.0
            return t.reshape(-1, 2).astype(np.float32)

        def _attn_mask(H, W):
            m = np.zeros((H, W), np.float32)
            hs = (slice(0, -WS[0]), slice(-WS[0], -SS[0]), slice(-SS[0], None))
            ws_ = (slice(0, -WS[1]), slice(-WS[1], -SS[1]), slice(-SS[1], None))
            cnt = 0
            for h in hs:
                for w in ws_:
                    m[h, w] = cnt
                    cnt += 1
            nWh, nWw = (H // WS[0], W // WS[1])
            m = m.reshape(nWh, WS[0], nWw, WS[1]).transpose(0, 2, 1, 3).reshape(nWh * nWw, WS[0] * WS[1])
            d = m[:, None, :] - m[:, :, None]
            return np.where(d != 0, -100.0, 0.0).astype(np.float32)

        def _layernorm(x, g, b):
            m = x.mean(-1, keepdims=True)
            v = x.var(-1, keepdims=True)
            return (x - m) / jnp.sqrt(v + 1e-05) * g + b

        def _shifted_window_attention(x, qkv_w, qkv_b, proj_w, proj_b, logit_scale, cpb_w1, cpb_b1, cpb_w2):
            B, H, W, C = x.shape
            nWh, nWw = (H // WS[0], W // WS[1])
            nW, N = (nWh * nWw, WS[0] * WS[1])
            xs = jnp.roll(x, (-SS[0], -SS[1]), axis=(1, 2))
            xw = xs.reshape(B, nWh, WS[0], nWw, WS[1], C).transpose(0, 1, 3, 2, 4, 5).reshape(B * nW, N, C)
            qkv_b = qkv_b.at[C:2 * C].set(0.0)
            qkv = xw @ qkv_w.T + qkv_b
            qkv = qkv.reshape(B * nW, N, 3, NUM_HEADS, HEAD_DIM).transpose(2, 0, 3, 1, 4)
            q, k, v = (qkv[0], qkv[1], qkv[2])
            qn = q / jnp.maximum(jnp.linalg.norm(q, axis=-1, keepdims=True), 1e-12)
            kn = k / jnp.maximum(jnp.linalg.norm(k, axis=-1, keepdims=True), 1e-12)
            attn = jnp.einsum('whnd,whmd->whnm', qn, kn)
            scale = jnp.exp(jnp.minimum(logit_scale, math.log(100.0)))
            attn = attn * scale[None]
            table = jax.nn.relu(jnp.asarray(_rel_coords_table()) @ cpb_w1.T + cpb_b1) @ cpb_w2.T
            bias = table[jnp.asarray(_rel_position_index())].reshape(N, N, NUM_HEADS).transpose(2, 0, 1)
            bias = 16.0 * jax.nn.sigmoid(bias)
            attn = attn + bias[None]
            mask = jnp.asarray(_attn_mask(H, W))
            attn = attn.reshape(B, nW, NUM_HEADS, N, N) + mask[None, :, None]
            attn = jax.nn.softmax(attn.reshape(B * nW, NUM_HEADS, N, N), axis=-1)
            out = jnp.einsum('whnm,whmd->whnd', attn, v).transpose(0, 2, 1, 3).reshape(B * nW, N, C)
            out = out @ proj_w.T + proj_b
            out = out.reshape(B, nWh, nWw, WS[0], WS[1], C).transpose(0, 1, 3, 2, 4, 5).reshape(B, H, W, C)
            return jnp.roll(out, (SS[0], SS[1]), axis=(1, 2))
        a = _shifted_window_attention(x, qkv_w, qkv_b, proj_w, proj_b, logit_scale, cpb_w1, cpb_b1, cpb_w2)
        x = x + _layernorm(a, norm1_g, norm1_b)
        h = jax.nn.gelu(x @ fc1_w.T + fc1_b, approximate=False) @ fc2_w.T + fc2_b
        x = x + _layernorm(h, norm2_g, norm2_b)
        return x

    def _L1_conv_ref(x, w_real, w_imag):
        import jax, jax.numpy as jnp
        import numpy as np
        KERNEL = 25
        NUM_MODES = 128

        def _moving_average(x, k):
            if k <= 1:
                return x
            left = k - 1 - (k - 1) // 2
            right = (k - 1) // 2
            xpad = jnp.concatenate([jnp.broadcast_to(x[:, :1], (x.shape[0], left) + x.shape[2:]), x, jnp.broadcast_to(x[:, -1:], (x.shape[0], right) + x.shape[2:])], axis=1)
            c = jnp.cumsum(xpad, axis=1)
            c = jnp.concatenate([jnp.zeros_like(c[:, :1]), c], axis=1)
            return (c[:, k:] - c[:, :-k]) / k
        B, T, N, C = x.shape
        M = w_real.shape[-1]
        trend = _moving_average(x, KERNEL)
        seasonal = x - trend
        xf = jnp.fft.rfft(seasonal, axis=1)
        xs = xf[:, :M]
        W = w_real + 1j * w_imag
        ys = jnp.einsum('bmnc,cmk->bknc', xs, W)
        F = T // 2 + 1
        yf = jnp.concatenate([ys, jnp.zeros((B, F - M, N, C), dtype=ys.dtype)], axis=1)
        filt = jnp.fft.irfft(yf, n=T, axis=1)
        return trend + filt

    def _gn(v, G=32, eps=1e-5):
        B_, H_, W_, C_ = v.shape
        g = v.reshape(B_, H_, W_, G, C_ // G)
        m = jnp.mean(g, axis=(1, 2, 4), keepdims=True)
        s = jnp.var(g, axis=(1, 2, 4), keepdims=True)
        return ((g - m) / jnp.sqrt(s + eps)).reshape(v.shape)

    def _ln_c(v, eps=1e-6):
        m = jnp.mean(v, axis=-1, keepdims=True)
        s = jnp.var(v, axis=-1, keepdims=True)
        return (v - m) / jnp.sqrt(s + eps)

    def _ln_t(v, eps=1e-5):
        m = jnp.mean(v, axis=-1, keepdims=True)
        s = jnp.var(v, axis=-1, keepdims=True)
        return (v - m) / jnp.sqrt(s + eps)

    def _to_tokens(v):
        B_, H_, W_, C_ = v.shape
        return v.reshape(B_, H_ * W_, C_)
    def _from_tokens(t, like):
        return t.reshape(like.shape)

    x = _L0_conv_ref(x, L0_conv_qkv_w, L0_conv_qkv_b, L0_conv_proj_w, L0_conv_proj_b, L0_conv_logit_scale, L0_conv_cpb_w1, L0_conv_cpb_b1, L0_conv_cpb_w2, L0_conv_norm1_g, L0_conv_norm1_b, L0_conv_norm2_g, L0_conv_norm2_b, L0_conv_fc1_w, L0_conv_fc1_b, L0_conv_fc2_w, L0_conv_fc2_b)
    x = _L1_conv_ref(x, L1_conv_w_real, L1_conv_w_imag)
    return x


_drawn_inputs = setup_inputs


def setup_inputs(seed=0):
    import zlib

    import numpy as np

    out = dict(_drawn_inputs(seed))
    spreads = {'L0_conv_qkv_b': (0.0, 0.1),
     'L0_conv_proj_b': (0.0, 0.1),
     'L0_conv_logit_scale': (2.3025851249694824, 0.2),
     'L0_conv_cpb_b1': (0.0, 0.8),
     'L0_conv_norm1_g': (1.0, 0.2),
     'L0_conv_norm1_b': (0.0, 0.1),
     'L0_conv_norm2_g': (1.0, 0.2),
     'L0_conv_norm2_b': (0.0, 0.1),
     'L0_conv_fc1_b': (0.0, 0.1),
     'L0_conv_fc2_b': (0.0, 0.1)}
    factors = {'L0_conv_cpb_w1': 8.0, 'L0_conv_cpb_w2': 8.0}
    for name, (base, spread) in spreads.items():
        noise = np.random.default_rng([zlib.crc32(name.encode()), seed]).standard_normal(out[name].shape)
        drawn = base * np.exp(spread * noise) if base else spread * noise
        out[name] = jnp.asarray(drawn.astype(out[name].dtype))
    for name, factor in factors.items():
        out[name] = (out[name] * factor).astype(out[name].dtype)
    return out
```

```python
from collections import namedtuple
from contextlib import ExitStack

import numpy as np
import concourse.bass as bass
from concourse import mybir

F32 = mybir.dt.float32
ALU = mybir.AluOpType
ACT = mybir.ActivationFunctionType
AX = mybir.AxisListType

P = 128
C = 64
HEADS, HD = 4, 16
WIN = 4
HID = 256
ROWS = 16
CPS = 8
SLOTS = 8
PAIRS = SLOTS // 2
GPS = 4
OFF = -30000.0
RELS = (2 * WIN - 1) ** 2
KERNEL = 25
MODES = 128
T = 256

Group = namedtuple("Group", "s off")


def shape_constants():
    ax = np.arange(-(WIN - 1), WIN, dtype=np.float32)
    t = np.stack(np.meshgrid(ax, ax, indexing="ij"), axis=-1)
    t /= WIN - 1
    t *= 8.0
    t = np.sign(t) * np.log2(np.abs(t) + 1.0) / 3.0
    coords = np.ascontiguousarray(t.reshape(-1, 2).astype(np.float32).T)
    pick = np.zeros((RELS + 1, 32, P), np.float32)
    for p in range(P):
        qi, qj = (p % 32) // CPS, p % CPS
        for m in range(32):
            ki, kj = m // CPS, m % CPS
            if qj // WIN == kj // WIN:
                pick[(qi - ki + WIN - 1) * (2 * WIN - 1) + (qj - kj + WIN - 1), m, p] = 1
            else:
                pick[RELS, m, p] = 1
    ma = np.zeros((T, T))
    for i in range(T):
        for j in range(i - KERNEL // 2, i + KERNEL // 2 + 1):
            ma[i, min(max(j, 0), T - 1)] += 1.0 / KERNEL
    s, m = np.arange(T), np.arange(MODES)
    ang = 2 * np.pi * ((m[:, None] * s[None, :]) % T) / T
    season = np.eye(T) - ma
    fr, fi = np.cos(ang) @ season, -np.sin(ang) @ season
    amp = np.where(m == 0, 1.0, 2.0)[:, None] / T
    cr, ci = amp * np.cos(ang), -amp * np.sin(ang)
    dft = np.concatenate([fr, fi, -fi, fr], axis=1)
    inverse = np.concatenate([cr, ci], axis=1)
    average = np.concatenate([ma.T[:P], ma.T[P:]], axis=1)
    return {"coords": coords, "pick": pick.reshape(RELS + 1, 32 * P),
            "dft": dft.astype(np.float32), "inverse": inverse.astype(np.float32),
            "average": average.astype(np.float32)}


def swin_then_fourier(nc, x, qkv_wt, qkv_b, proj_wt, proj_b, logit_scale, cpb_w1t, cpb_b1, cpb_w2t,
                      n1g, n1b, n2g, n2b, fc1_wt, fc1_b, fc2_wt, fc2_b, w_real, w_imag,
                      coords, pick, dft, inverse, average, out, y, mix):
    B, H, W, _ = x.shape
    NS = B * H // ROWS
    G = NS * GPS
    BL1, NCH = out.shape[0], C
    HALF = W // 2
    GC = HALF // GPS
    xr = x.rearrange("b h w c -> (b h) w c")
    yr = y.rearrange("b h c w -> (b h) c w")

    with ExitStack() as ctx:
        def sb(name, cols):
            return ctx.enter_context(nc.sbuf_tensor(name, [P, cols], F32))

        def sem(name):
            return ctx.enter_context(nc.semaphore(name))

        ps = ctx.enter_context(nc.psum_tensor("ps", [P, 8, 512], F32))
        arena = sb("arena", 2 * T * C)
        used = [0]

        def carve(cols):
            a = used[0]
            used[0] += cols
            assert used[0] <= 2 * T * C
            return arena[:, a:a + cols]

        ident = carve(P)
        wqkv = carve(2 * 3 * C).rearrange("p (a n) -> p a n", a=2)
        wproj = carve(C)
        w1 = carve(2 * HID).rearrange("p (a n) -> p a n", a=2)
        b1 = carve(2)
        w2 = carve(2 * C).rearrange("p (k n) -> p k n", k=2)
        bqkv = carve(3 * C)
        g1, o1, g2, o2, b2 = (carve(C) for _ in range(5))
        scale = carve(HEADS)
        eps = carve(1)
        relb = carve(HEADS * 32).rearrange("p (h m) -> p h m", h=HEADS)
        picks = carve(32 * P).rearrange("p (m q) -> p m q", m=32)
        cw1, cco = carve(512), carve(RELS)
        cb1 = carve(4)
        cw2 = carve(4 * HEADS).rearrange("p (k h) -> p k h", k=4)
        hid = carve(4 * RELS).rearrange("p (k r) -> p k r", k=4)
        table = carve(HEADS)
        SC = SLOTS * C
        xin = [carve(SC).rearrange("p (s c) -> p s c", s=SLOTS) for _ in range(2)]
        xo1 = [carve(SC) for _ in range(2)]
        xT = [carve(PAIRS * P).rearrange("p (s n) -> p s n", s=PAIRS) for _ in range(2)]
        qkv = carve(SLOTS * 3 * C).rearrange("p (s n) -> p s n", s=SLOTS)
        sq = carve(SLOTS * 2 * C)
        ss, rt, rn = (carve(SLOTS * 2 * HEADS) for _ in range(3))
        qkn = carve(SLOTS * 2 * P).rearrange("p (s k h d) -> p s k h d", s=SLOTS, k=2, h=HEADS)
        qkT = carve(SLOTS * 2 * P).rearrange("p (s k n) -> p s k n", s=SLOTS, k=2)
        vpad = [carve(SLOTS * P).rearrange("p (s h d) -> p s h d", s=SLOTS, h=HEADS) for _ in range(2)]
        prob = carve(HEADS * SLOTS * 32).rearrange("p (h s m) -> p h s m", h=HEADS, s=SLOTS)
        mx, sm, rs = (carve(HEADS * SLOTS) for _ in range(3))
        probT = carve(HEADS * SLOTS * 32).rearrange("p (h s n) -> p h s n", h=HEADS, s=SLOTS)
        oT = carve(SLOTS * P).rearrange("p (s g n) -> p s g n", s=SLOTS, g=4)
        nd, nsq = [carve(SC) for _ in range(2)], [carve(SC) for _ in range(2)]
        lsum, lssq, lrt, lrs = ([carve(SLOTS) for _ in range(2)] for _ in range(4))
        x1 = [carve(SC) for _ in range(2)]
        x1o2 = [carve(SC) for _ in range(2)]
        x1T = carve(PAIRS * P)
        hT = carve(2 * 2 * 512).rearrange("p (a k n) -> p a k n", a=2, k=2)
        h2 = carve(SC)
        yo = carve(SC)
        ystripe = carve(ROWS * HALF).rearrange("p (r q n) -> p r q n", r=ROWS, q=GPS)
        NB = 4
        dftm, invm, avgm = sb("dftm", 1024), sb("invm", 512), sb("avgm", 512)
        wri = [sb(f"wri{i}", 2 * P) for i in range(2)]
        vri = [sb(f"vri{i}", 512) for i in range(2)]
        amat = [sb(f"amat{i}", 512) for i in range(NB)]
        xch = [sb(f"xch{i}", 512) for i in range(NB)]
        orow = arena[:, :].rearrange("p (k n c) -> p k n c", k=2, c=C)

        att = ps[:, 0:4, :]
        S = att[:, :, 0:256].rearrange("p h (s m) -> p h s m", m=32)
        PV = att[:, :, 256:512].rearrange("p g (s n) -> p g s n", n=32)
        mmb = [ps[:, 4, :], ps[:, 5, :]]
        acc, tr = ps[:, 6, :], ps[:, 7, :]

        consts, made, set_up, made_id = sem("consts"), sem("made"), sem("set_up"), sem("made_id")
        x_in = [sem("x_in0"), sem("x_in1")]
        xT_ps, xT_sb = sem("xT_ps"), sem("xT_sb")
        qkv_ps, qkv_sb = sem("qkv_ps"), sem("qkv_sb")
        squared, summed = sem("squared"), sem("summed")
        rooted, factor = sem("rooted"), sem("factor")
        qk_norm, v_put, xo_put = sem("qk_norm"), sem("v_put"), sem("xo_put")
        qkT_ps, qkT_sb = sem("qkT_ps"), sem("qkT_sb")
        S_ps, biased, maxed, shifted = sem("S_ps"), sem("biased"), sem("maxed"), sem("shifted")
        exped, prob_sum, probs, probT_sb = sem("exped"), sem("prob_sum"), sem("probs"), sem("probT_sb")
        pv_ps, oT_sb, proj_ps = sem("pv_ps"), sem("oT_sb"), sem("proj_ps")
        ln1_d, ln1_sq, ln1_ss, ln1_rt, ln1_n = (sem(f"ln1_{n}") for n in ("d", "sq", "ss", "rt", "n"))
        ln2_d, ln2_sq, ln2_ss, ln2_rt, ln2_n = (sem(f"ln2_{n}") for n in ("d", "sq", "ss", "rt", "n"))
        x1_sb, x1T_ps, x1T_sb = sem("x1_sb"), sem("x1T_ps"), sem("x1T_sb")
        fc1_ps, gelued, fc2_ps = sem("fc1_ps"), sem("gelued"), sem("fc2_ps")
        y_sb, yT_ps, yT_sb, y_out = sem("y_sb"), sem("yT_ps"), sem("yT_sb"), sem("y_out")
        w_in = [sem("w_in0"), sem("w_in1")]
        v_ps, v_sb, m_ps, m_sb = sem("v_ps"), sem("v_sb"), sem("m_ps"), sem("m_sb")
        m_out = [sem(f"m_out{i}") for i in range(NB)]
        ch_in = [sem(f"ch_in{i}") for i in range(NB)]
        o_ps, o_act, o_dve, rows_out = sem("o_ps"), sem("o_act"), sem("o_dve"), sem("rows_out")

        def there(g):
            return not isinstance(g.s, int) or 0 <= g.s * GPS + g.off < G

        def need(eng, s, per, g, n):
            if there(g):
                eng.wait_ge(s, g.s * (GPS * per) + (g.off * per + n))

        def over_groups(eng, step):
            for k in range(GPS):
                step(0, k)
            if NS > 1:
                with eng.Fori(1, NS) as s:
                    for k in range(GPS):
                        step(s, k)
            for k in range(2):
                step(NS, k)

        def row(t):
            return t.unsqueeze(1).to_broadcast([P, SLOTS, C])

        def slots(t):
            return t.rearrange("p (s c) -> p s c", s=SLOTS)

        def per_slot(t):
            return t.unsqueeze(2).to_broadcast([P, SLOTS, C])

        consts_in = 16 * 27
        block = ctx.enter_context(nc.Block())

        @block.sync
        def _(sp):
            n = [0]

            def const(dst, src):
                n[0] += 1
                sp.dma_start(dst, src).then_inc(consts, 16)

            sp.wait_ge(set_up, 6)
            for a in range(2):
                const(wqkv[a * C:a * C + C, a, :], qkv_wt)
                const(w1[a * C:a * C + C, a, :], fc1_wt)
            for h in range(HEADS):
                const(wproj[32 * h:32 * h + HD, :], proj_wt[h * HD:h * HD + HD, :])
            const(wproj[HD:HD + 1, :], proj_b)
            const(b1, fc1_b)
            const(w2, fc2_wt.rearrange("(k p) n -> p k n", k=2))
            const(scale, logit_scale.partition_broadcast(P))
            const(bqkv[:, 0:C], qkv_b[0, 0:C].partition_broadcast(P))
            const(bqkv[:, 2 * C:3 * C], qkv_b[0, 2 * C:3 * C].partition_broadcast(P))
            for dst, src in ((g1, n1g), (o1, n1b), (g2, n2g), (o2, n2b), (b2, fc2_b)):
                const(dst, src[0, :].partition_broadcast(P))
            const(picks[0:RELS + 1], pick.rearrange("r (m q) -> r m q", m=32))
            const(cw1[0:2, :], cpb_w1t)
            const(cco[0:2, :], coords)
            const(cb1, cpb_b1)
            const(cw2, cpb_w2t.rearrange("(k p) h -> p k h", k=4))
            const(dftm[:, :], dft)
            const(invm[:, :], inverse)
            const(avgm[:, :], average)
            assert 16 * n[0] == consts_in

            def mix_loads(c2, j, first):
                if not first:
                    sp.wait_ge(v_ps, c2 * 2 + (j - 1))
                sp.dma_start(wri[j][:, 0:P], w_real[bass.ds(c2 * 2 + j, 1)].rearrange("a m k -> (a m) k")).then_inc(w_in[j], 16)
                sp.dma_start(wri[j][:, P:2 * P], w_imag[bass.ds(c2 * 2 + j, 1)].rearrange("a m k -> (a m) k")).then_inc(w_in[j], 16)

            def mix_store(c2, j):
                sp.wait_ge(m_sb, c2 * 2 + j + 1)
                sp.dma_start(mix[bass.ds(c2 * 2 + j, 1)].rearrange("a p n -> (a p) n"), amat[j][:, :]).then_inc(m_out[j], 16)

            mix_loads(0, 0, True)
            mix_loads(0, 1, True)
            with sp.Fori(1, NCH // 2) as c2:
                for j in range(2):
                    mix_loads(c2, j, False)
                for j in range(2):
                    mix_store(c2 - 1, j)
            for j in range(2):
                mix_store(NCH // 2 - 1, j)

            def load_x(g):
                par = g.off % 2
                q = g.off % GPS
                need(sp, xT_ps, 1, Group(g.s, g.off - 2), 1)
                need(sp, xo_put, 1, Group(g.s, g.off - 2), 1)
                src = xr[bass.ds(g.s * ROWS, ROWS)] if g.off < GPS else xr[bass.ds((g.s + 1) * ROWS, ROWS)]
                for sl in range(SLOTS):
                    c0 = (sl % 2) * HALF + q * GC + (sl // 2) * CPS
                    sp.dma_start(xin[par][:, sl, :], src[:, c0:c0 + CPS, :]).then_inc(x_in[par], 16)

            def store_y(s):
                need(sp, yT_sb, 1, Group(s, GPS - 1), 1)
                for a in range(2):
                    sp.dma_start(
                        yr[bass.ds(s * ROWS, ROWS), :, a * HALF:(a + 1) * HALF].rearrange("r c n -> c r n"),
                        ystripe[a * C:(a + 1) * C].rearrange("p r q n -> p r (q n)")).then_inc(y_out, 16)

            load_x(Group(0, 0))
            load_x(Group(0, 1))

            def step(s, k):
                if k < 2 or not isinstance(s, int) or s < NS - 1:
                    if there(Group(s, k + 2)):
                        load_x(Group(s, k + 2))
                if k == 1 and not (isinstance(s, int) and s == 0):
                    store_y(s - 1)

            for k in range(GPS):
                step(0, k)
            if NS > 2:
                with sp.Fori(1, NS - 1) as s:
                    for k in range(GPS):
                        step(s, k)
            if NS > 1:
                for k in range(GPS):
                    step(NS - 1, k)
            step(NS, 0)
            step(NS, 1)
            sp.wait_ge(y_out, 32 * NS)
            for j in range(2):
                sp.wait_ge(m_out[j], 16 * (NCH // 2))

            def channel_in(b, cq, j, before):
                if before is not None:
                    sp.wait_ge(o_ps, before)
                c = cq * NB + j
                sp.dma_start(amat[j][:, :], mix[bass.ds(c, 1)].rearrange("a p n -> (a p) n")).then_inc(ch_in[j], 16)
                sp.dma_start(xch[j][:, :].rearrange("p (k n) -> p k n", k=2),
                             y[b].rearrange("(k t) c n -> t k c n", k=2)[:, :, bass.ds(c, 1), :].rearrange("t k c n -> t k (c n)")).then_inc(ch_in[j], 16)

            for b in range(BL1):
                for j in range(NB):
                    channel_in(b, 0, j, b * NCH + j + 1 - NB if b else None)
                with sp.Fori(1, NCH // NB) as cq:
                    for j in range(NB):
                        channel_in(b, cq, j, cq * NB + (b * NCH + j + 1 - NB))

        @block.tensor
        def _(pe):
            mm = pe.matmul
            pe.wait_ge(consts, consts_in)
            for k in range(4):
                mm(acc[:, k * RELS:(k + 1) * RELS], cw1[0:2, k * P:(k + 1) * P], cco[0:2, :],
                   start=True, stop=True).then_inc(made, 1)
            pe.wait_ge(set_up, 7)
            for k in range(4):
                ins = mm(tr[0:RELS, 0:HEADS], hid[:, k, :], cw2[:, k, :], start=(k == 0), stop=(k == 3))
            ins.then_inc(made, 1)
            pe.wait_ge(set_up, 9)
            for m in range(32):
                ins = mm(acc.rearrange("p (m h) -> p m h", h=HEADS)[:, m, :], picks[0:RELS + 1, m, :],
                         table[0:RELS + 1, :], start=True, stop=True)
            ins.then_inc(made, 1)

            def mix_step(c2, j, first):
                pe.wait_ge(w_in[j], c2 * 32 + 32)
                if not first:
                    pe.wait_ge(v_sb, c2 * 2 + (j - 1))
                mm(mmb[j], wri[j][:, 0:P], dftm[:, 0:512], start=True, stop=False)
                mm(mmb[j], wri[j][:, P:2 * P], dftm[:, 512:1024], start=False, stop=True).then_inc(v_ps, 1)

            def mix_step2(c2, j, first):
                pe.wait_ge(v_sb, c2 * 2 + j + 1)
                if not first:
                    pe.wait_ge(m_sb, c2 * 2 + (j - 1))
                for k in range(2):
                    for r in range(2):
                        ins = mm(ps[:, j, k * T:(k + 1) * T], vri[j][:, r * T + k * P:r * T + (k + 1) * P],
                                 invm[:, r * T:(r + 1) * T], start=(r == 0), stop=(r == 1))
                ins.then_inc(m_ps, 1)

            for j in range(2):
                mix_step(0, j, True)
            for j in range(2):
                mix_step2(0, j, True)
            with pe.Fori(1, NCH // 2) as c2:
                for j in range(2):
                    mix_step(c2, j, False)
                for j in range(2):
                    mix_step2(c2, j, False)
            pe.wait_ge(m_sb, NCH)
            pe.wait_ge(set_up, 10)
            pe.wait_ge(made_id, 7)

            def step(s, k):
                i0, i1, i2 = Group(s, k), Group(s, k - 1), Group(s, k - 2)
                par = k % 2
                if there(i0):
                    pe.wait_ge(x_in[par], s * (2 * SLOTS * 16) + (k // 2 + 1) * SLOTS * 16)
                    need(pe, x1T_sb, 1, i1._replace(off=k - 2), 1)
                    for p in range(PAIRS):
                        ins = pe.transpose(tr[:, p * P:(p + 1) * P],
                                           xin[par][:, 2 * p:2 * p + 2, :].rearrange("p s c -> p (s c)"), ident)
                    ins.then_inc(xT_ps, 1)
                if there(i2):
                    need(pe, x1T_sb, 1, i2, 1)
                    for j in range(4):
                        if j < 2:
                            need(pe, qkT_sb, 4, i1, 3 + j)
                        else:
                            need(pe, gelued, 4, i2, j - 1)
                        mm(mmb[j % 2], w1[:, j // 2, (j % 2) * P:(j % 2 + 1) * P], x1T,
                           start=True, stop=True).then_inc(fc1_ps, 1)
                if there(i0):
                    need(pe, xT_sb, 1, i0, 1)
                    for p in range(PAIRS):
                        if p < 2:
                            need(pe, gelued, 4, i2, 3 + p)
                            if not there(i2):
                                need(pe, qkT_sb, 4, i1, 3 + p)
                        else:
                            need(pe, qkv_sb, 4, i0, p - 1)
                        mm(mmb[p % 2][:, 0:6 * C], xT[par][:, p, :], wqkv.rearrange("p a n -> p (a n)"),
                           start=True, stop=True).then_inc(qkv_ps, 1)
                if there(i2):
                    need(pe, gelued, 4, i2, 4)
                    for sl in range(SLOTS):
                        for kk in range(2):
                            ins = mm(acc[:, sl * C:(sl + 1) * C],
                                     hT[:, sl % 2, kk, (sl // 2) * P:(sl // 2 + 1) * P], w2[:, kk, :],
                                     start=(kk == 0), stop=(kk == 1))
                    ins.then_inc(fc2_ps, 1)
                if there(i1):
                    pe.wait_ge(made_id, 7)
                    need(pe, probT_sb, 1, i1, 1)
                    need(pe, v_put, 1, i1, 1)
                    need(pe, oT_sb, 1, i2, 1)
                    vp = vpad[(k - 1) % 2]
                    for sl in range(SLOTS):
                        for g in range(4):
                            for h in range(HEADS):
                                ins = mm(PV[32 * h:32 * h + 32, g, sl, :], vp[32 * g:32 * g + 32, sl, h, :],
                                         probT[32 * g:32 * g + 32, h, sl, :], start=True, stop=True,
                                         tile_position=(32 * g, 32 * h))
                    ins.then_inc(pv_ps, 1)

                def qk_transposed(f):
                    if f < 2:
                        need(pe, qk_norm, 1, i0, 1)
                        need(pe, qkv_sb, 4, i0, 3 + f)
                    else:
                        need(pe, qkT_sb, 4, i0, f - 1)
                    for j in range(4):
                        ins = pe.transpose(mmb[f % 2][:, j * P:(j + 1) * P],
                                           qkn[:, 2 * f + j // 2, j % 2, :, :].rearrange("p h d -> p (h d)"), ident)
                    ins.then_inc(qkT_ps, 1)

                if there(i0):
                    qk_transposed(0)
                    qk_transposed(1)
                if there(i1):
                    need(pe, oT_sb, 1, i1, 1)
                    need(pe, ln2_d, 3, i2, 1)
                    for sl in range(SLOTS):
                        ins = mm(acc[:, sl * C:(sl + 1) * C], oT[:, sl, :, :].rearrange("p g n -> p (g n)"), wproj,
                                 start=True, stop=True)
                    ins.then_inc(proj_ps, 1)
                if there(i0):
                    qk_transposed(2)
                    qk_transposed(3)
                if there(i2):
                    need(pe, y_sb, 2, i2, 2)
                    need(pe, xT_sb, 1, i0, 1)
                    if not there(i0):
                        need(pe, x1T_sb, 1, i2, 1)
                    for p in range(PAIRS):
                        ins = pe.transpose(tr[:, p * P:(p + 1) * P], yo[:, p * P:(p + 1) * P], ident)
                    ins.then_inc(yT_ps, 1)

                def scores(sl):
                    pe.wait_ge(made_id, 7)
                    need(pe, qkT_sb, 4, i0, sl // 2 + 1)
                    if sl == 0:
                        need(pe, biased, 1, i1, 1)
                    for h in range(HEADS):
                        for g in range(4):
                            ins = mm(S[32 * g:32 * g + 32, h, sl, :],
                                     qkT[32 * h:32 * h + HD, sl, 0, 32 * g:32 * g + 32],
                                     qkT[32 * h:32 * h + HD, sl, 1, 32 * g:32 * g + 32],
                                     start=True, stop=True, tile_position=(32 * h, 32 * g))
                    if sl == SLOTS - 1:
                        ins.then_inc(S_ps, 1)

                if there(i0):
                    for sl in range(SLOTS - 2):
                        scores(sl)
                if there(i1):
                    need(pe, x1_sb, 3, i1, 2)
                    need(pe, yT_sb, 1, i2, 1)
                    need(pe, xT_sb, 1, i0, 1)
                    for p in range(PAIRS):
                        ins = pe.transpose(tr[:, p * P:(p + 1) * P], x1[(k - 1) % 2][:, p * P:(p + 1) * P], ident)
                    ins.then_inc(x1T_ps, 1)
                if there(i0):
                    for sl in range(SLOTS - 2, SLOTS):
                        scores(sl)

            over_groups(pe, step)

            def channel(b, cq, j, first):
                pe.wait_ge(ch_in[j], cq * 32 + (b * (NCH // NB) + 1) * 32)
                if not first:
                    pe.wait_ge(o_dve if j % 2 else o_act, cq * 2 + (b * (NCH // 2) + j // 2 - 1))
                for k in range(2):
                    for r in range(2):
                        ins = mm(ps[:, j, k * T:(k + 1) * T], amat[j][:, r * T + k * P:r * T + (k + 1) * P],
                                 xch[j][:, r * T:(r + 1) * T], start=(r == 0), stop=(r == 1))
                ins.then_inc(o_ps, 1)

            for b in range(BL1):
                for j in range(NB):
                    channel(b, 0, j, b == 0)
                with pe.Fori(1, NCH // NB) as cq:
                    for j in range(NB):
                        channel(b, cq, j, False)

        @block.scalar
        def _(act):
            f = act.activation
            act.wait_ge(consts, consts_in)
            act.wait_ge(set_up, 8)
            f(table[0:RELS, :], table[0:RELS, :], ACT.Sigmoid).then_inc(set_up, 1)
            act.wait_ge(set_up, 11)
            f(scale, scale, ACT.Exp).then_inc(set_up, 1)

            def mix_step(c2, j, first):
                act.wait_ge(v_ps, c2 * 2 + j + 1)
                if not first:
                    act.wait_ge(m_ps, c2 * 2 + (j - 1))
                f(vri[j][:, :], mmb[j], ACT.Copy).then_inc(v_sb, 1)

            for j in range(2):
                mix_step(0, j, True)
            with act.Fori(1, NCH // 2) as c2:
                for j in range(2):
                    mix_step(c2, j, False)

            def step(s, k):
                i0, i1, i2 = Group(s, k), Group(s, k - 1), Group(s, k - 2)
                par = k % 2
                if there(i0):
                    need(act, xT_ps, 1, i0, 1)
                    f(xT[par].rearrange("p s n -> p (s n)"), tr, ACT.Copy).then_inc(xT_sb, 1)
                if there(i2):
                    for j in range(4):
                        need(act, fc1_ps, 4, i2, j + 1)
                        if j == 0:
                            need(act, fc2_ps, 1, i2._replace(off=k - 3), 1)
                        f(hT[:, j // 2, j % 2, :], mmb[j % 2], ACT.Gelu, bias=b1[:, j % 2:j % 2 + 1]).then_inc(gelued, 1)
                if there(i1):
                    need(act, shifted, 1, i1, 1)
                    pr = prob.rearrange("p h s m -> p (h s m)")
                    f(pr, pr, ACT.Exp).then_inc(exped, 1)
                if there(i0):
                    need(act, qkv_sb, 4, i0, 4)
                    need(act, summed, 2, i1, 1)
                    f(sq.rearrange("p (s n) -> p s n", s=SLOTS), qkv[:, :, 0:2 * C], ACT.Square).then_inc(squared, 1)
                    need(act, summed, 2, i0, 2)
                    need(act, factor, 2, i1, 1)
                    f(rt, ss, ACT.Sqrt).then_inc(rooted, 1)

                def norm_root(g, kk, d, sqd, ssd, rtd, nn, last, prev):
                    need(act, d, last, g, last)
                    need(act, ssd, 1, prev, 1)
                    f(nsq[kk], nd[kk], ACT.Square).then_inc(sqd, 1)
                    need(act, ssd, 1, g, 1)
                    need(act, nn, 2, prev, 1)
                    f(lrt[kk], lssq[kk], ACT.Sqrt, scale=1.0 / C, bias=eps).then_inc(rtd, 1)

                if there(i2):
                    norm_root(i2, 1, ln2_d, ln2_sq, ln2_ss, ln2_rt, ln2_n, 3, Group(s, k - 3))
                if there(i1):
                    need(act, pv_ps, 1, i1, 1)
                    need(act, proj_ps, 1, i2, 1)
                    f(oT.rearrange("p s g n -> p g s n"), PV, ACT.Copy).then_inc(oT_sb, 1)
                if there(i0):
                    for j in range(4):
                        need(act, qkT_ps, 4, i0, j + 1)
                        if j == 0:
                            need(act, S_ps, 1, i1, 1)
                        f(qkT[:, 2 * j:2 * j + 2, :, :].rearrange("p s k n -> p (s k n)"), mmb[j % 2],
                          ACT.Copy).then_inc(qkT_sb, 1)
                if there(i1):
                    norm_root(i1, 0, ln1_d, ln1_sq, ln1_ss, ln1_rt, ln1_n, 2, Group(s, k - 2))
                if there(i2):
                    need(act, yT_ps, 1, i2, 1)
                    q = (k - 2) % GPS
                    if q == 0 and not (isinstance(s, int) and s == 0):
                        act.wait_ge(y_out, s * 32)
                    f(ystripe[:, :, q, :].rearrange("p r (i j) -> p i r j", j=CPS),
                      tr.rearrange("p (i r j) -> p i r j", i=PAIRS, j=CPS), ACT.Copy).then_inc(yT_sb, 1)
                if there(i1):
                    need(act, x1T_ps, 1, i1, 1)
                    f(x1T, tr, ACT.Copy).then_inc(x1T_sb, 1)

            over_groups(act, step)

            def put(b, cq, j):
                act.wait_ge(o_ps, cq * NB + (b * NCH + j + 1))
                f(orow[:, :, :, bass.ds(cq * NB + j, 1)].rearrange("p k n c -> p (k n) c"),
                  ps[:, j, :].unsqueeze(2), ACT.Copy).then_inc(o_act, 1)

            act.wait_ge(y_out, 32 * NS)
            for b in range(BL1):
                if b:
                    act.wait_ge(rows_out, 64 * b)
                with act.Fori(0, NCH // NB) as cq:
                    for j in (0, 2):
                        put(b, cq, j)
                act.wait_ge(o_dve, (b + 1) * NCH // 2)
                act.wait_ge(o_act, (b + 1) * NCH // 2)
                for k in range(2):
                    for hh in range(2):
                        act.dma_start(out[b, k * P:(k + 1) * P, hh * 128:(hh + 1) * 128, :].rearrange("t n c -> t (n c)"),
                                      orow[:, k, hh * 128:(hh + 1) * 128, :].rearrange("p n c -> p (n c)"))\
                            .then_inc(rows_out, 16)
            act.wait_ge(rows_out, 64 * BL1)

        @block.vector
        def _(dve):
            tt, ts = dve.tensor_tensor, dve.tensor_scalar
            dve.memset(wqkv, 0.0).then_inc(set_up, 1)
            dve.memset(wproj, 0.0).then_inc(set_up, 1)
            dve.memset(w1, 0.0).then_inc(set_up, 1)
            dve.memset(bqkv, 0.0).then_inc(set_up, 1)
            dve.memset(table, OFF / 16).then_inc(set_up, 1)
            dve.memset(eps, 1e-5).then_inc(set_up, 1)
            dve.wait_ge(consts, consts_in)
            dve.wait_ge(made, 4)
            for k in range(4):
                ins = ts(hid[:, k, :], acc[:, k * RELS:(k + 1) * RELS], cb1[:, k:k + 1], 0.0, ALU.add, ALU.max)
            ins.then_inc(set_up, 1)
            dve.wait_ge(made, 5)
            dve.wait_ge(set_up, 7)
            dve.tensor_copy(table[0:RELS, :], tr[0:RELS, 0:HEADS]).then_inc(set_up, 1)
            dve.wait_ge(made, 6)
            ts(relb.rearrange("p h m -> p m h"), acc[:, 0:P].rearrange("p (m h) -> p m h", h=HEADS),
               16.0, None, ALU.mult).then_inc(set_up, 1)
            dve.wait_ge(set_up, 10)
            ts(scale, scale, float(np.float32(np.log(100.0))), None, ALU.min).then_inc(set_up, 1)
            dve.wait_ge(set_up, 12)

            def mix_step(c2, j, first):
                dve.wait_ge(m_ps, c2 * 2 + j + 1)
                if not first:
                    dve.wait_ge(m_out[j], c2 * 16)
                tt(amat[j][:, :], ps[:, j, :], avgm[:, :], ALU.add).then_inc(m_sb, 1)

            for j in range(2):
                mix_step(0, j, True)
            with dve.Fori(1, NCH // 2) as c2:
                for j in range(2):
                    mix_step(c2, j, False)

            pr3 = prob.rearrange("p h s m -> p (h s) m")

            def step(s, k):
                i0, i1, i2, i3 = (Group(s, k - d) for d in range(4))

                def qkv_bias(p):
                    need(dve, qkv_ps, 4, i0, p + 1)
                    if p == 0:
                        need(dve, qk_norm, 1, i1, 1)
                        need(dve, v_put, 1, i1, 1)
                        need(dve, squared, 1, i1, 1)
                    tt(qkv[:, 2 * p:2 * p + 2, :], mmb[p % 2][:, 0:6 * C].rearrange("p (s n) -> p s n", s=2),
                       bqkv.unsqueeze(1).to_broadcast([P, 2, 3 * C]), ALU.add).then_inc(qkv_sb, 1)

                if there(i1):
                    need(dve, S_ps, 1, i1, 1)
                    need(dve, probT_sb, 1, i2, 1)
                    tt(prob, S, relb.unsqueeze(2).to_broadcast([P, HEADS, SLOTS, 32]), ALU.add).then_inc(biased, 1)
                    need(dve, biased, 1, i1, 1)
                    need(dve, shifted, 1, i2, 1)
                    dve.tensor_reduce(mx, pr3, AX.X, ALU.max).then_inc(maxed, 1)
                if there(i0):
                    qkv_bias(0)
                    qkv_bias(1)
                if there(i1):
                    need(dve, exped, 1, i1, 1)
                    dve.tensor_reduce(sm, pr3, AX.X, ALU.add).then_inc(prob_sum, 1)
                    need(dve, prob_sum, 2, i1, 1)
                    need(dve, probs, 1, i2, 1)
                    dve.reciprocal(rs, sm).then_inc(prob_sum, 1)
                if there(i0):
                    qkv_bias(2)
                    qkv_bias(3)
                    need(dve, squared, 1, i0, 1)
                    need(dve, rooted, 1, i1, 1)
                    dve.tensor_reduce(ss, sq.rearrange("p (n d) -> p n d", d=HD), AX.X, ALU.add).then_inc(summed, 1)
                    need(dve, summed, 2, i0, 1)
                    ts(ss, ss, 1e-24, None, ALU.max).then_inc(summed, 1)
                if there(i1):
                    need(dve, probs, 1, i1, 1)
                    need(dve, pv_ps, 1, i2, 1)
                    dve.transpose(probT.rearrange("p h s n -> p (h s n)"),
                                  prob.rearrange("p h s m -> p (h s m)")).then_inc(probT_sb, 1)
                if there(i0):
                    need(dve, rooted, 1, i0, 1)
                    need(dve, qk_norm, 1, i1, 1)
                    dve.reciprocal(rn, rt).then_inc(factor, 1)
                    need(dve, factor, 2, i0, 1)
                    rq = rn.rearrange("p (s k h) -> p s k h", s=SLOTS, k=2)[:, :, 0, :]
                    tt(rq, rq, scale.unsqueeze(1).to_broadcast([P, SLOTS, HEADS]), ALU.mult).then_inc(factor, 1)

                def norm_sums(src, g, kk, d, n0, last, sq_prev, prev):
                    dve.tensor_reduce(lsum[kk], slots(src), AX.X, ALU.add).then_inc(d, 1)
                    need(dve, d, last, g, n0 + 1)
                    dve.scalar_tensor_tensor(slots(nd[kk]), per_slot(lsum[kk]), 1.0 / C, slots(src),
                                             ALU.mult, ALU.subtract).then_inc(d, 1)

                def norm_scale(g, kk, sqd, ssd, rtd, nn, prev):
                    need(dve, sqd, 1, g, 1)
                    dve.tensor_reduce(lssq[kk], slots(nsq[kk]), AX.X, ALU.add).then_inc(ssd, 1)
                    need(dve, rtd, 1, g, 1)
                    dve.reciprocal(lrs[kk], lrt[kk]).then_inc(nn, 1)
                    need(dve, nn, 2, g, 1)
                    tt(slots(nd[kk]), slots(nd[kk]), per_slot(lrs[kk]), ALU.mult).then_inc(nn, 1)

                if there(i2):
                    need(dve, fc2_ps, 1, i2, 1)
                    tt(slots(h2), slots(acc), row(b2), ALU.add).then_inc(ln2_d, 1)
                    need(dve, ln2_d, 3, i2, 1)
                    need(dve, y_sb, 2, i3, 2)
                    norm_sums(h2, i2, 1, ln2_d, 1, 3, None, None)
                    norm_scale(i2, 1, ln2_sq, ln2_ss, ln2_rt, ln2_n, i3)
                if there(i1):
                    need(dve, proj_ps, 1, i1, 1)
                    need(dve, x1_sb, 3, i2, 2)
                    norm_sums(acc, i1, 0, ln1_d, 0, 2, None, None)
                    norm_scale(i1, 0, ln1_sq, ln1_ss, ln1_rt, ln1_n, i2)

            over_groups(dve, step)

            def put(b, cq, j):
                dve.wait_ge(o_ps, cq * NB + (b * NCH + j + 1))
                dve.tensor_copy(orow[:, :, :, bass.ds(cq * NB + j, 1)].rearrange("p k n c -> p (k n) c"),
                                ps[:, j, :].unsqueeze(2)).then_inc(o_dve, 1)

            dve.wait_ge(y_out, 32 * NS)
            for b in range(BL1):
                if b:
                    dve.wait_ge(rows_out, 64 * b)
                with dve.Fori(0, NCH // NB) as cq:
                    for j in (1, 3):
                        put(b, cq, j)

        @block.gpsimd
        def _(pool):
            tt = pool.tensor_tensor
            pool.memset(ident, 0.0).then_inc(made_id, 1)
            pool.wait_ge(made_id, 1)
            pool.affine_select(out=ident, in_=ident, compare_op=ALU.not_equal, fill=1.0, base=0,
                               pattern=[[-1, P]], channel_multiplier=1).then_inc(made_id, 1)
            pool.memset(qkn, 0.0).then_inc(made_id, 1)
            for v in vpad:
                pool.memset(v, 0.0).then_inc(made_id, 1)
            pool.wait_ge(made_id, 5)
            for v in vpad:
                pool.memset(v[:, :, :, HD:HD + 1], 1.0).then_inc(made_id, 1)
            pool.wait_ge(made_id, 7)
            pool.wait_ge(consts, consts_in)

            def step(s, k):
                i0, i1, i2, i3 = (Group(s, k - d) for d in range(4))
                par = k % 2
                hs = HEADS * SLOTS
                pr3 = prob.rearrange("p h s m -> p (h s) m")
                if there(i1):
                    need(pool, maxed, 1, i1, 1)
                    tt(pr3, pr3, mx.unsqueeze(2).to_broadcast([P, hs, 32]), ALU.subtract).then_inc(shifted, 1)
                if there(i0):
                    pool.wait_ge(x_in[par], s * (2 * SLOTS * 16) + (k // 2 + 1) * SLOTS * 16)
                    tt(slots(xo1[par]), xin[par], row(o1), ALU.add).then_inc(xo_put, 1)
                if there(i1):
                    need(pool, prob_sum, 2, i1, 2)
                    tt(pr3, pr3, rs.unsqueeze(2).to_broadcast([P, hs, 32]), ALU.mult).then_inc(probs, 1)
                if there(i0):
                    need(pool, factor, 2, i0, 2)
                    need(pool, qkT_ps, 4, i1, 4)
                    need(pool, pv_ps, 1, i2, 1)
                    tt(qkn.rearrange("p s k h d -> p (s k h) d")[:, :, 0:HD],
                       qkv[:, :, 0:2 * C].rearrange("p s (n d) -> p s n d", d=HD),
                       rn.unsqueeze(2).to_broadcast([P, SLOTS * 2 * HEADS, HD]), ALU.mult).then_inc(qk_norm, 1)
                    pool.tensor_copy(vpad[par][:, :, :, 0:HD],
                                     qkv[:, :, 2 * C:3 * C].rearrange("p s (h d) -> p s h d", d=HD)).then_inc(v_put, 1)
                if there(i2):
                    kk = (k - 2) % 2
                    need(pool, ln2_n, 2, i2, 2)
                    need(pool, yT_ps, 1, i3, 1)
                    tt(slots(nd[1]), slots(nd[1]), row(g2), ALU.mult).then_inc(y_sb, 1)
                    need(pool, y_sb, 2, i2, 1)
                    tt(yo, x1o2[kk], nd[1], ALU.subtract).then_inc(y_sb, 1)
                if there(i1):
                    kk = (k - 1) % 2
                    need(pool, ln1_n, 2, i1, 2)
                    need(pool, x1T_ps, 1, i3, 1)
                    tt(slots(nd[0]), slots(nd[0]), row(g1), ALU.mult).then_inc(x1_sb, 1)
                    need(pool, x1_sb, 3, i1, 1)
                    tt(x1[kk], xo1[kk], nd[0], ALU.subtract).then_inc(x1_sb, 1)
                    need(pool, x1_sb, 3, i1, 2)
                    tt(slots(x1o2[kk]), slots(x1[kk]), row(o2), ALU.add).then_inc(x1_sb, 1)

            over_groups(pool, step)


def arrays_of(inputs):
    L0, L1 = "L0_conv_", "L1_conv_"
    t = lambda n: np.ascontiguousarray(np.asarray(inputs[L0 + n]).T)
    row = lambda n: np.asarray(inputs[L0 + n]).reshape(1, -1)
    cols = lambda n: np.ascontiguousarray(np.asarray(inputs[L0 + n]).reshape(-1, P).T)
    a = {"x": np.asarray(inputs["x"]), "qkv_wt": t("qkv_w"), "qkv_b": row("qkv_b"), "proj_wt": t("proj_w"),
         "proj_b": row("proj_b"), "logit_scale": np.asarray(inputs[L0 + "logit_scale"]).reshape(-1),
         "cpb_w1t": t("cpb_w1"), "cpb_b1": cols("cpb_b1"), "cpb_w2t": t("cpb_w2"),
         "n1g": row("norm1_g"), "n1b": row("norm1_b"), "n2g": row("norm2_g"), "n2b": row("norm2_b"),
         "fc1_wt": t("fc1_w"), "fc1_b": cols("fc1_b"), "fc2_wt": t("fc2_w"), "fc2_b": row("fc2_b"),
         "w_real": np.asarray(inputs[L1 + "w_real"]), "w_imag": np.asarray(inputs[L1 + "w_imag"])}
    a.update(shape_constants())
    return a


def kernel(**inputs):
    import concourse.bacc as _bacc
    from concourse.bass_utils import run_bass_kernel_spmd as _run

    nc = _bacc.Bacc("TRN2", target_bir_lowering=False, num_devices=1)
    arrays, args = {}, []
    for name, a in arrays_of(inputs).items():
        arrays[f"in_{name}"] = a
        args.append(nc.dram_tensor(f"in_{name}", a.shape, F32, kind="ExternalInput").ap())
    shape = tuple(inputs["x"].shape)
    args.append(nc.dram_tensor("out", shape, F32, kind="ExternalOutput").ap())
    b, h, w, c = shape
    args.append(nc.dram_tensor("y", (b, h, c, w), F32, kind="Internal").ap())
    args.append(nc.dram_tensor("mix", (C, P, 2 * T), F32, kind="Internal").ap())
    swin_then_fourier(nc, *args)
    r = _run(nc, [arrays], core_ids=[0])
    return r.results[0]["out"]
```

```python
from collections import namedtuple
from contextlib import ExitStack

import numpy as np
import concourse.bass as bass
from concourse import mybir

F32 = mybir.dt.float32
ALU = mybir.AluOpType
ACT = mybir.ActivationFunctionType
AX = mybir.AxisListType

P = 128
C = 64
HEADS, HD = 4, 16
WIN = 4
HID = 256
ROWS = 16
CPS = 8
SLOTS = 8
PAIRS = SLOTS // 2
GPS = 4
LAG = 5
PEEL = 2
OFF = -30000.0
RELS = (2 * WIN - 1) ** 2
KERNEL = 25
MODES = 128
T = 256

Group = namedtuple("Group", "s off")


def shape_constants():
    ax = np.arange(-(WIN - 1), WIN, dtype=np.float32)
    t = np.stack(np.meshgrid(ax, ax, indexing="ij"), axis=-1)
    t /= WIN - 1
    t *= 8.0
    t = np.sign(t) * np.log2(np.abs(t) + 1.0) / 3.0
    coords = np.ascontiguousarray(t.reshape(-1, 2).astype(np.float32).T)
    pick = np.zeros((RELS + 1, 32, P), np.float32)
    for p in range(P):
        qi, qj = (p % 32) // CPS, p % CPS
        for m in range(32):
            ki, kj = m // CPS, m % CPS
            if qj // WIN == kj // WIN:
                pick[(qi - ki + WIN - 1) * (2 * WIN - 1) + (qj - kj + WIN - 1), m, p] = 1
            else:
                pick[RELS, m, p] = 1
    ma = np.zeros((T, T))
    for i in range(T):
        for j in range(i - KERNEL // 2, i + KERNEL // 2 + 1):
            ma[i, min(max(j, 0), T - 1)] += 1.0 / KERNEL
    s, m = np.arange(T), np.arange(MODES)
    ang = 2 * np.pi * ((m[:, None] * s[None, :]) % T) / T
    season = np.eye(T) - ma
    fr, fi = np.cos(ang) @ season, -np.sin(ang) @ season
    amp = np.where(m == 0, 1.0, 2.0)[:, None] / T
    cr, ci = amp * np.cos(ang), -amp * np.sin(ang)
    dft = np.concatenate([fr, fi, -fi, fr], axis=1)
    inverse = np.concatenate([cr, ci], axis=1)
    average = np.concatenate([ma.T[:P], ma.T[P:]], axis=1)
    return {"coords": coords, "pick": pick.reshape(RELS + 1, 32 * P),
            "dft": dft.astype(np.float32), "inverse": inverse.astype(np.float32),
            "average": average.astype(np.float32)}


def swin_then_fourier(nc, x, qkv_wt, qkv_b, v_b, proj_wt, proj_b, logit_scale, cpb_w1t, cpb_b1, cpb_w2t,
                      n1g, n1b, n2g, n2b, fc1_wt, fc1_b, fc2_wt, fc2_b, w_real, w_imag,
                      coords, pick, dft, inverse, average, out, y, mix):
    B, H, W, _ = x.shape
    NS = B * H // ROWS
    G = NS * GPS
    BL1, NCH = out.shape[0], C
    HALF = W // 2
    GC = HALF // GPS
    xr = x.rearrange("b h w c -> (b h) w c")
    yr = y.rearrange("b h c w -> (b h) c w")

    with ExitStack() as ctx:
        def sb(name, cols):
            return ctx.enter_context(nc.sbuf_tensor(name, [P, cols], F32))

        def sem(name):
            return ctx.enter_context(nc.semaphore(name))

        ps = ctx.enter_context(nc.psum_tensor("ps", [P, 8, 512], F32))
        arena = sb("arena", 2 * T * C)
        used = [0]

        def carve(cols):
            a = used[0]
            used[0] += cols
            assert used[0] <= 2 * T * C
            return arena[:, a:a + cols]

        ident = carve(P)
        wqkv = carve(2 * 3 * C).rearrange("p (a n) -> p a n", a=2)
        wproj = carve(C)
        w1 = carve(2 * HID).rearrange("p (a n) -> p a n", a=2)
        b1 = carve(2)
        w2 = carve(2 * C).rearrange("p (k n) -> p k n", k=2)
        bqk = carve(2 * C)
        bvcol, pickb, wproj2 = carve(1), carve(P), carve(C)
        g1, o1, g2, o2, b2 = (carve(C) for _ in range(5))
        scale = carve(HEADS)
        eps, warm = carve(1), carve(3)
        relb = carve(HEADS * 32).rearrange("p (h m) -> p h m", h=HEADS)
        picks = carve(32 * P).rearrange("p (m q) -> p m q", m=32)
        cw1, cco = carve(512), carve(RELS)
        cb1 = carve(4)
        cw2 = carve(4 * HEADS).rearrange("p (k h) -> p k h", k=4)
        hid = carve(4 * RELS).rearrange("p (k r) -> p k r", k=4)
        table = carve(HEADS)
        SC = SLOTS * C
        xin = [carve(SC).rearrange("p (s c) -> p s c", s=SLOTS) for _ in range(2)]
        xo1 = [carve(SC) for _ in range(4)]
        xT = carve(PAIRS * P).rearrange("p (s n) -> p s n", s=PAIRS)
        qk = carve(SLOTS * 2 * C).rearrange("p (s n) -> p s n", s=SLOTS)
        sq = carve(SLOTS * 2 * C)
        ss, rt, rn = (carve(SLOTS * 2 * HEADS) for _ in range(3))
        qkn = carve(SLOTS * 2 * P).rearrange("p (s k h d) -> p s k h d", s=SLOTS, k=2, h=HEADS)
        qkT = carve(SLOTS * 2 * P).rearrange("p (s k n) -> p s k n", s=SLOTS, k=2)
        vpad = [sb(f"vpad{i}", SLOTS * P)[:, :].rearrange("p (s h d) -> p s h d", s=SLOTS, h=HEADS)
                for i in range(4)]
        prob = carve(HEADS * SLOTS * 32).rearrange("p (h s m) -> p h s m", h=HEADS, s=SLOTS)
        mx, sm, rs = (carve(HEADS * SLOTS) for _ in range(3))
        probT = carve(HEADS * SLOTS * 32).rearrange("p (h s n) -> p h s n", h=HEADS, s=SLOTS)
        oT = carve(SLOTS * P).rearrange("p (s g n) -> p s g n", s=SLOTS, g=4)
        nd, nsq = [carve(SC) for _ in range(2)], [carve(SC) for _ in range(2)]
        lsum, lssq, lrt, lrs = ([carve(SLOTS) for _ in range(2)] for _ in range(4))
        x1 = carve(SC)
        x1o2 = [carve(SC) for _ in range(2)]
        x1T = carve(PAIRS * P)
        hT = carve(2 * 2 * 512).rearrange("p (a k n) -> p a k n", a=2, k=2)
        h2 = carve(SC)
        yo = carve(SC)
        ystripe = carve(ROWS * HALF).rearrange("p (r q n) -> p r q n", r=ROWS, q=GPS)
        NB = 4
        dftm, invm, avgm = sb("dftm", 1024), sb("invm", 512), sb("avgm", 512)
        wri = [sb(f"wri{i}", 2 * P) for i in range(2)]
        vri = [sb(f"vri{i}", 512) for i in range(2)]
        amat = [sb(f"amat{i}", 512) for i in range(NB)]
        xch = [sb(f"xch{i}", 512) for i in range(NB)]
        orow = arena[:, :].rearrange("p (k n c) -> p k n c", k=2, c=C)

        att = ps[:, 0:4, :]
        S = att[:, :, 0:256].rearrange("p h (s m) -> p h s m", m=32)
        PV = att[:, :, 256:512].rearrange("p g (s n) -> p g s n", n=32)
        mmb = [ps[:, 4, :], ps[:, 5, :]]
        acc, tr = ps[:, 6, :], ps[:, 7, :]

        consts, made, set_up = sem("consts"), sem("made"), sem("set_up")
        made_id, pick_made = sem("made_id"), sem("pick_made")
        x_in = [sem("x_in0"), sem("x_in1")]
        xT_ps, xT_sb = sem("xT_ps"), sem("xT_sb")
        qkv_ps, qkv_sb = sem("qkv_ps"), sem("qkv_sb")
        squared, summed = sem("squared"), sem("summed")
        rooted, factor = sem("rooted"), sem("factor")
        qk_norm, v_put, xo_put = sem("qk_norm"), sem("v_put"), sem("xo_put")
        qkT_ps, qkT_sb = sem("qkT_ps"), sem("qkT_sb")
        S_ps, biased, maxed, shifted = sem("S_ps"), sem("biased"), sem("maxed"), sem("shifted")
        exped, prob_sum, probs, probT_sb = sem("exped"), sem("prob_sum"), sem("probs"), sem("probT_sb")
        pv_ps, oT_sb, proj_ps = sem("pv_ps"), sem("oT_sb"), sem("proj_ps")
        ln1_d, ln1_sq, ln1_ss, ln1_rt, ln1_n = (sem(f"ln1_{n}") for n in ("d", "sq", "ss", "rt", "n"))
        ln2_d, ln2_sq, ln2_ss, ln2_rt, ln2_n = (sem(f"ln2_{n}") for n in ("d", "sq", "ss", "rt", "n"))
        x1_sb, x1T_ps, x1T_sb = sem("x1_sb"), sem("x1T_ps"), sem("x1T_sb")
        fc1_ps, gelued, fc2_ps = sem("fc1_ps"), sem("gelued"), sem("fc2_ps")
        y_sb, yT_ps, yT_sb, y_out = sem("y_sb"), sem("yT_ps"), sem("yT_sb"), sem("y_out")
        w_in = [sem("w_in0"), sem("w_in1")]
        v_ps, v_sb, m_ps, m_sb = sem("v_ps"), sem("v_sb"), sem("m_ps"), sem("m_sb")
        m_out = [sem(f"m_out{i}") for i in range(NB)]
        ch_in = [sem(f"ch_in{i}") for i in range(NB)]
        o_ps, o_act, o_dve, rows_out = sem("o_ps"), sem("o_act"), sem("o_dve"), sem("rows_out")

        def there(g):
            return not isinstance(g.s, int) or 0 <= g.s * GPS + g.off < G

        def need(eng, s, per, g, n):
            if there(g):
                eng.wait_ge(s, g.s * (GPS * per) + (g.off * per + n))

        def over_groups(eng, step):
            for i in range(PEEL * GPS):
                step(i // GPS, i % GPS)
            with eng.Fori(PEEL, NS) as s:
                for k in range(GPS):
                    step(s, k)
            for i in range(LAG):
                step(NS + i // GPS, i % GPS)

        last = Group(NS - 1, GPS - 1)

        def row(t):
            return t.unsqueeze(1).to_broadcast([P, SLOTS, C])

        def slots(t):
            return t.rearrange("p (s c) -> p s c", s=SLOTS)

        def per_slot(t):
            return t.unsqueeze(2).to_broadcast([P, SLOTS, C])

        consts_in = 16 * 30
        block = ctx.enter_context(nc.Block())

        @block.sync
        def _(sp):
            n = [0]

            def const(dst, src):
                n[0] += 1
                sp.dma_start(dst, src).then_inc(consts, 16)

            sp.wait_ge(set_up, 7)
            for a in range(2):
                const(wqkv[a * C:a * C + C, a, :], qkv_wt)
                const(w1[a * C:a * C + C, a, :], fc1_wt)
            for h in range(HEADS):
                const(wproj[32 * h:32 * h + HD, :], proj_wt[h * HD:h * HD + HD, :])
            const(wproj[HD:HD + 1, :], proj_b)
            const(b1, fc1_b)
            const(w2, fc2_wt.rearrange("(k p) n -> p k n", k=2))
            const(scale, logit_scale.partition_broadcast(P))
            const(bqk[:, 0:C], qkv_b[0, 0:C].partition_broadcast(P))
            for h in range(HEADS):
                const(bvcol[32 * h:32 * h + HD, :], v_b[h * HD:h * HD + HD, :])
            for dst, src in ((g1, n1g), (o1, n1b), (g2, n2g), (o2, n2b), (b2, fc2_b)):
                const(dst, src[0, :].partition_broadcast(P))
            const(picks[0:RELS + 1], pick.rearrange("r (m q) -> r m q", m=32))
            const(cw1[0:2, :], cpb_w1t)
            const(cco[0:2, :], coords)
            const(cb1, cpb_b1)
            const(cw2, cpb_w2t.rearrange("(k p) h -> p k h", k=4))
            const(dftm[:, :], dft)
            const(invm[:, :], inverse)
            const(avgm[:, :], average)
            assert 16 * n[0] == consts_in

            def mix_loads(c2, j, first):
                if not first:
                    sp.wait_ge(v_ps, c2 * 2 + (j - 1))
                sp.dma_start(wri[j][:, 0:P], w_real[bass.ds(c2 * 2 + j, 1)].rearrange("a m k -> (a m) k")).then_inc(w_in[j], 16)
                sp.dma_start(wri[j][:, P:2 * P], w_imag[bass.ds(c2 * 2 + j, 1)].rearrange("a m k -> (a m) k")).then_inc(w_in[j], 16)

            def mix_store(c2, j):
                sp.wait_ge(m_sb, c2 * 2 + j + 1)
                sp.dma_start(mix[bass.ds(c2 * 2 + j, 1)].rearrange("a p n -> (a p) n"), amat[j][:, :]).then_inc(m_out[j], 16)

            mix_loads(0, 0, True)
            mix_loads(0, 1, True)
            with sp.Fori(1, NCH // 2) as c2:
                for j in range(2):
                    mix_loads(c2, j, False)
                for j in range(2):
                    mix_store(c2 - 1, j)
            for j in range(2):
                mix_store(NCH // 2 - 1, j)

            def load_x(g):
                par = g.off % 2
                q = g.off % GPS
                need(sp, xT_ps, 1, Group(g.s, g.off - 2), 1)
                need(sp, xo_put, 1, Group(g.s, g.off - 2), 1)
                src = xr[bass.ds(g.s * ROWS, ROWS)] if g.off < GPS else xr[bass.ds((g.s + 1) * ROWS, ROWS)]
                for sl in range(SLOTS):
                    c0 = (sl % 2) * HALF + q * GC + (sl // 2) * CPS
                    sp.dma_start(xin[par][:, sl, :], src[:, c0:c0 + CPS, :]).then_inc(x_in[par], 16)

            def store_y(s):
                need(sp, yT_sb, 1, Group(s, GPS - 1), 1)
                for a in range(2):
                    sp.dma_start(
                        yr[bass.ds(s * ROWS, ROWS), :, a * HALF:(a + 1) * HALF].rearrange("r c n -> c r n"),
                        ystripe[a * C:(a + 1) * C].rearrange("p r q n -> p r (q n)")).then_inc(y_out, 16)

            load_x(Group(0, 0))
            load_x(Group(0, 1))

            def step(s, k):
                if k < 2 or not isinstance(s, int) or s < NS - 1:
                    if there(Group(s, k + 2)):
                        load_x(Group(s, k + 2))
                if k == 0 and not (isinstance(s, int) and s < 2):
                    store_y(s - 2)

            for i in range(PEEL * GPS):
                step(i // GPS, i % GPS)
            with sp.Fori(PEEL, NS - 1) as s:
                for k in range(GPS):
                    step(s, k)
            for i in range(GPS + LAG):
                step(NS - 1 + i // GPS, i % GPS)
            sp.wait_ge(y_out, 32 * NS)
            for j in range(2):
                sp.wait_ge(m_out[j], 16 * (NCH // 2))

            def channel_in(b, cq, j, before):
                if before is not None:
                    sp.wait_ge(o_ps, before)
                c = cq * NB + j
                sp.dma_start(amat[j][:, :], mix[bass.ds(c, 1)].rearrange("a p n -> (a p) n")).then_inc(ch_in[j], 16)
                sp.dma_start(xch[j][:, :].rearrange("p (k n) -> p k n", k=2),
                             y[b].rearrange("(k t) c n -> t k c n", k=2)[:, :, bass.ds(c, 1), :].rearrange("t k c n -> t k (c n)")).then_inc(ch_in[j], 16)

            for b in range(BL1):
                for j in range(NB):
                    channel_in(b, 0, j, b * NCH + j + 1 - NB if b else None)
                with sp.Fori(1, NCH // NB) as cq:
                    for j in range(NB):
                        channel_in(b, cq, j, cq * NB + (b * NCH + j + 1 - NB))

        @block.tensor
        def _(pe):
            mm = pe.matmul
            pe.wait_ge(consts, consts_in)
            for k in range(4):
                mm(acc[:, k * RELS:(k + 1) * RELS], cw1[0:2, k * P:(k + 1) * P], cco[0:2, :],
                   start=True, stop=True).then_inc(made, 1)
            pe.wait_ge(set_up, 8)
            for k in range(4):
                ins = mm(tr[0:RELS, 0:HEADS], hid[:, k, :], cw2[:, k, :], start=(k == 0), stop=(k == 3))
            ins.then_inc(made, 1)
            pe.wait_ge(set_up, 10)
            for m in range(32):
                ins = mm(acc.rearrange("p (m h) -> p m h", h=HEADS)[:, m, :], picks[0:RELS + 1, m, :],
                         table[0:RELS + 1, :], start=True, stop=True)
            ins.then_inc(made, 1)
            pe.wait_ge(made_id, 12)
            mm(tr[:, 0:C], pickb, wproj, start=True, stop=True).then_inc(made, 1)

            def mix_step(c2, j, first):
                pe.wait_ge(w_in[j], c2 * 32 + 32)
                if not first:
                    pe.wait_ge(v_sb, c2 * 2 + (j - 1))
                mm(mmb[j], wri[j][:, 0:P], dftm[:, 0:512], start=True, stop=False)
                mm(mmb[j], wri[j][:, P:2 * P], dftm[:, 512:1024], start=False, stop=True).then_inc(v_ps, 1)

            def mix_step2(c2, j, first):
                pe.wait_ge(v_sb, c2 * 2 + j + 1)
                if not first:
                    pe.wait_ge(m_sb, c2 * 2 + (j - 1))
                for k in range(2):
                    for r in range(2):
                        ins = mm(ps[:, j, k * T:(k + 1) * T], vri[j][:, r * T + k * P:r * T + (k + 1) * P],
                                 invm[:, r * T:(r + 1) * T], start=(r == 0), stop=(r == 1))
                ins.then_inc(m_ps, 1)

            for j in range(2):
                mix_step(0, j, True)
            for j in range(2):
                mix_step2(0, j, True)
            with pe.Fori(1, NCH // 2) as c2:
                for j in range(2):
                    mix_step(c2, j, False)
                for j in range(2):
                    mix_step2(c2, j, False)
            pe.wait_ge(m_sb, NCH)
            pe.wait_ge(set_up, 14)
            pe.wait_ge(made_id, 11)

            def step(s, k):
                i0, i1, i2, i3, i4, i5, i6 = (Group(s, k - d) for d in range(7))
                par = k % 2

                def turn(dst, tiles, done):
                    for j, t in enumerate(tiles):
                        ins = pe.transpose(dst[:, j * P:(j + 1) * P], t, ident)
                    ins.then_inc(done, 1)

                def scores(sl):
                    for h in range(HEADS):
                        for g in range(4):
                            ins = mm(S[32 * g:32 * g + 32, h, sl, :],
                                     qkT[32 * h:32 * h + HD, sl, 0, 32 * g:32 * g + 32],
                                     qkT[32 * h:32 * h + HD, sl, 1, 32 * g:32 * g + 32],
                                     start=True, stop=True, tile_position=(32 * h, 32 * g))
                    if sl == SLOTS - 1:
                        ins.then_inc(S_ps, 1)

                def weighted(sl):
                    for g in range(4):
                        for h in range(HEADS):
                            ins = mm(PV[32 * h:32 * h + 32, g, sl, :], vpad[(k - 2) % 4][32 * g:32 * g + 32, sl, h, :],
                                     probT[32 * g:32 * g + 32, h, sl, :], start=True, stop=True,
                                     tile_position=(32 * g, 32 * h))
                    if sl == SLOTS - 1:
                        ins.then_inc(pv_ps, 1)

                def second_layer(p):
                    if p == 0:
                        need(pe, gelued, 4, i4, 4)
                        need(pe, ln1_d, 2, i3, 2)
                        if not there(i3):
                            need(pe, ln2_d, 3, i5, 1)
                    for sl in (2 * p, 2 * p + 1):
                        for kk in range(2):
                            ins = mm(acc[:, sl * C:(sl + 1) * C],
                                     hT[:, sl % 2, kk, (sl // 2) * P:(sl // 2 + 1) * P], w2[:, kk, :],
                                     start=(kk == 0), stop=(kk == 1))
                    if p == PAIRS - 1:
                        ins.then_inc(fc2_ps, 1)

                def qk_turned(f):
                    if f == 0:
                        need(pe, qk_norm, 1, i1, 1)
                    if f < 2:
                        need(pe, gelued, 4, i4, 3 + f)
                        if not there(i4):
                            need(pe, v_put, 4, i1, 3 + f)
                    else:
                        need(pe, qkT_sb, 4, i1, f - 1)
                    turn(mmb[f % 2], [qkn[:, 2 * f + j // 2, j % 2, :, :].rearrange("p h d -> p (h d)")
                                      for j in range(4)], qkT_ps)

                def project(p):
                    if p == 0:
                        need(pe, oT_sb, 1, i3, 1)
                        need(pe, ln2_d, 3, i5, 1)
                        if not there(i5):
                            need(pe, ln1_d, 2, i4, 2)
                    for sl in (2 * p, 2 * p + 1):
                        ins = mm(acc[:, sl * C:(sl + 1) * C], oT[:, sl, :, :].rearrange("p g n -> p (g n)"),
                                 wproj2, start=True, stop=True)
                    if p == PAIRS - 1:
                        ins.then_inc(proj_ps, 1)

                def qkv(p):
                    if p == 0:
                        need(pe, xT_sb, 1, i0, 1)
                    if p < 2:
                        need(pe, qkT_sb, 4, i1, 3 + p)
                    else:
                        need(pe, v_put, 4, i0, p - 1)
                    mm(mmb[p % 2][:, 0:6 * C], xT[:, p, :], wqkv.rearrange("p a n -> p (a n)"),
                       start=True, stop=True).then_inc(qkv_ps, 1)

                def first_layer(j):
                    if j == 0:
                        need(pe, x1T_sb, 1, i3, 1)
                    if j < 2:
                        need(pe, v_put, 4, i0, 3 + j)
                        if not there(i0):
                            need(pe, qkT_sb, 4, i1, 3 + j)
                            need(pe, gelued, 4, i4, 3 + j)
                    else:
                        need(pe, gelued, 4, i3, j - 1)
                    mm(mmb[j % 2], w1[:, j // 2, (j % 2) * P:(j % 2 + 1) * P], x1T,
                       start=True, stop=True).then_inc(fc1_ps, 1)

                if there(i0):
                    pe.wait_ge(x_in[par], s * (2 * SLOTS * 16) + (k // 2 + 1) * SLOTS * 16)
                    need(pe, yT_sb, 1, i6, 1)
                    if not there(i6):
                        need(pe, x1T_sb, 1, i4, 1)
                        need(pe, xT_sb, 1, i1, 1)
                    turn(tr, [xin[par][:, 2 * p:2 * p + 2, :].rearrange("p s c -> p (s c)")
                              for p in range(PAIRS)], xT_ps)
                if there(i1):
                    qk_turned(0)
                    qk_turned(1)
                if there(i3):
                    project(0)
                    project(1)
                if there(i1):
                    qk_turned(2)
                if there(i3):
                    project(2)
                if there(i1):
                    qk_turned(3)
                if there(i3):
                    project(3)
                if there(i0):
                    qkv(0)
                if there(i1):
                    need(pe, qkT_sb, 4, i1, 4)
                    need(pe, oT_sb, 1, i3, 1)
                    if not there(i3):
                        need(pe, biased, 1, i2, 1)
                if there(i0):
                    qkv(1)
                if there(i1):
                    scores(0)
                    scores(1)
                if there(i0):
                    qkv(2)
                    qkv(3)
                for p in range(PAIRS):
                    if p == PAIRS - 1 and there(i3):
                        need(pe, x1_sb, 3, i3, 2)
                        need(pe, xT_sb, 1, i0, 1)
                        if not there(i0):
                            need(pe, yT_sb, 1, i6, 1)
                        turn(tr, [x1[:, q * P:(q + 1) * P] for q in range(PAIRS)], x1T_ps)
                    if there(i4):
                        second_layer(p)
                    if p < PAIRS - 1 and there(i1):
                        scores(2 * p + 2)
                        scores(2 * p + 3)
                if there(i3):
                    first_layer(0)
                if there(i2):
                    need(pe, biased, 1, i1, 1)
                    need(pe, probT_sb, 1, i2, 1)
                    need(pe, v_put, 4, i2, 4)
                if there(i3):
                    first_layer(1)
                for p in range(PAIRS):
                    if there(i2):
                        weighted(2 * p)
                        weighted(2 * p + 1)
                    if p in (1, 2) and there(i3):
                        first_layer(p + 1)
                    if p == 2 and there(i5):
                        need(pe, y_sb, 2, i5, 2)
                        need(pe, x1T_sb, 1, i3, 1)
                        if not there(i3):
                            need(pe, yT_sb, 1, i6, 1)
                        turn(tr, [yo[:, q * P:(q + 1) * P] for q in range(PAIRS)], yT_ps)

            over_groups(pe, step)

            def channel(b, cq, j, first):
                pe.wait_ge(ch_in[j], cq * 32 + (b * (NCH // NB) + 1) * 32)
                if not first:
                    pe.wait_ge(o_dve if j % 2 else o_act, cq * 2 + (b * (NCH // 2) + j // 2 - 1))
                for k in range(2):
                    for r in range(2):
                        ins = mm(ps[:, j, k * T:(k + 1) * T], amat[j][:, r * T + k * P:r * T + (k + 1) * P],
                                 xch[j][:, r * T:(r + 1) * T], start=(r == 0), stop=(r == 1))
                ins.then_inc(o_ps, 1)

            for b in range(BL1):
                for j in range(NB):
                    channel(b, 0, j, b == 0)
                with pe.Fori(1, NCH // NB) as cq:
                    for j in range(NB):
                        channel(b, cq, j, False)

        @block.scalar
        def _(act):
            f = act.activation
            act.wait_ge(consts, consts_in)
            act.wait_ge(set_up, 9)
            f(table[0:RELS, :], table[0:RELS, :], ACT.Sigmoid).then_inc(set_up, 1)
            act.wait_ge(set_up, 12)
            f(scale, scale, ACT.Exp).then_inc(set_up, 1)

            def mix_step(c2, j, first):
                act.wait_ge(v_ps, c2 * 2 + j + 1)
                if not first:
                    act.wait_ge(m_ps, c2 * 2 + (j - 1))
                f(vri[j][:, :], mmb[j], ACT.Copy).then_inc(v_sb, 1)

            for j in range(2):
                mix_step(0, j, True)
            with act.Fori(1, NCH // 2) as c2:
                for j in range(2):
                    mix_step(c2, j, False)

            def step(s, k):
                i0, i1, i2, i3, i4, i5, i6 = (Group(s, k - d) for d in range(7))
                par = k % 2

                def norm_square(g, kk, d, sqd, ssd, last, prev):
                    need(act, d, last, g, last)
                    need(act, ssd, 1, prev, 1)
                    f(nsq[kk], nd[kk], ACT.Square).then_inc(sqd, 1)

                def norm_root(g, kk, ssd, rtd, nn, prev):
                    need(act, ssd, 1, g, 1)
                    need(act, nn, 2, prev, 2)
                    f(lrt[kk], lssq[kk], ACT.Sqrt, scale=1.0 / C, bias=eps).then_inc(rtd, 1)

                def load_table(i, func):
                    f(warm[:, i:i + 1], eps, func)

                if there(i3):
                    need(act, pv_ps, 1, i3, 1)
                    need(act, proj_ps, 1, i4, 1)
                    f(oT.rearrange("p s g n -> p g s n"), PV, ACT.Copy).then_inc(oT_sb, 1)
                if there(i0):
                    need(act, xT_ps, 1, i0, 1)
                    f(xT.rearrange("p s n -> p (s n)"), tr, ACT.Copy).then_inc(xT_sb, 1)
                if there(i1):
                    for j in range(4):
                        need(act, qkT_ps, 4, i1, j + 1)
                        if j == 0:
                            need(act, S_ps, 1, i2, 1)
                        f(qkT[:, 2 * j:2 * j + 2, :, :].rearrange("p s k n -> p (s k n)"), mmb[j % 2],
                          ACT.Copy).then_inc(qkT_sb, 1)
                if there(i2):
                    need(act, shifted, 1, i2, 1)
                    pr = prob.rearrange("p h s m -> p (h s m)")
                    f(pr, pr, ACT.Exp).then_inc(exped, 1)
                if there(i3):
                    norm_square(i3, 0, ln1_d, ln1_sq, ln1_ss, 2, i4)
                load_table(1, ACT.Sqrt)
                if there(i0):
                    need(act, qkv_sb, 4, i0, 4)
                    need(act, summed, 2, i1, 1)
                    f(sq, qk.rearrange("p s n -> p (s n)"), ACT.Square).then_inc(squared, 1)
                if there(i5):
                    norm_root(i5, 1, ln2_ss, ln2_rt, ln2_n, i6)
                if there(i3):
                    norm_root(i3, 0, ln1_ss, ln1_rt, ln1_n, i4)
                if there(i0):
                    need(act, summed, 2, i0, 2)
                    need(act, factor, 2, i1, 1)
                    f(rt, ss, ACT.Sqrt).then_inc(rooted, 1)
                if there(i3):
                    load_table(2, ACT.Gelu)
                    for j in range(4):
                        need(act, fc1_ps, 4, i3, j + 1)
                        if j == 0:
                            need(act, fc2_ps, 1, i4, 1)
                        f(hT[:, j // 2, j % 2, :], mmb[j % 2], ACT.Gelu, bias=b1[:, j % 2:j % 2 + 1]).then_inc(gelued, 1)
                if there(i1):
                    load_table(0, ACT.Exp)
                if there(i4):
                    norm_square(i4, 1, ln2_d, ln2_sq, ln2_ss, 3, i5)

            over_groups(act, step)

            def put(b, cq, j):
                act.wait_ge(o_ps, cq * NB + (b * NCH + j + 1))
                f(orow[:, :, :, bass.ds(cq * NB + j, 1)].rearrange("p k n c -> p (k n) c"),
                  ps[:, j, :].unsqueeze(2), ACT.Copy).then_inc(o_act, 1)

            act.wait_ge(y_out, 32 * NS)
            for b in range(BL1):
                if b:
                    act.wait_ge(rows_out, 64 * b)
                with act.Fori(0, NCH // NB) as cq:
                    for j in (0, 2):
                        put(b, cq, j)
                act.wait_ge(o_dve, (b + 1) * NCH // 2)
                act.wait_ge(o_act, (b + 1) * NCH // 2)
                for k in range(2):
                    for hh in range(2):
                        act.dma_start(out[b, k * P:(k + 1) * P, hh * 128:(hh + 1) * 128, :].rearrange("t n c -> t (n c)"),
                                      orow[:, k, hh * 128:(hh + 1) * 128, :].rearrange("p n c -> p (n c)"))\
                            .then_inc(rows_out, 16)
            act.wait_ge(rows_out, 64 * BL1)

        @block.vector
        def _(dve):
            tt, ts = dve.tensor_tensor, dve.tensor_scalar
            dve.memset(wqkv, 0.0).then_inc(set_up, 1)
            dve.memset(wproj, 0.0).then_inc(set_up, 1)
            dve.memset(w1, 0.0).then_inc(set_up, 1)
            dve.memset(bqk, 0.0).then_inc(set_up, 1)
            dve.memset(bvcol, 0.0).then_inc(set_up, 1)
            dve.memset(table, OFF / 16).then_inc(set_up, 1)
            dve.memset(eps, 1e-5).then_inc(set_up, 1)
            dve.wait_ge(consts, consts_in)
            dve.wait_ge(made, 4)
            for k in range(4):
                ins = ts(hid[:, k, :], acc[:, k * RELS:(k + 1) * RELS], cb1[:, k:k + 1], 0.0, ALU.add, ALU.max)
            ins.then_inc(set_up, 1)
            dve.wait_ge(made, 5)
            dve.wait_ge(set_up, 8)
            dve.tensor_copy(table[0:RELS, :], tr[0:RELS, 0:HEADS]).then_inc(set_up, 1)
            dve.wait_ge(made, 6)
            ts(relb.rearrange("p h m -> p m h"), acc[:, 0:P].rearrange("p (m h) -> p m h", h=HEADS),
               16.0, None, ALU.mult).then_inc(set_up, 1)
            dve.wait_ge(set_up, 11)
            ts(scale, scale, float(np.float32(np.log(100.0))), None, ALU.min).then_inc(set_up, 1)
            dve.wait_ge(set_up, 13)
            dve.wait_ge(made, 7)
            dve.tensor_copy(wproj2, tr[:, 0:C]).then_inc(set_up, 1)

            def mix_step(c2, j, first):
                dve.wait_ge(m_ps, c2 * 2 + j + 1)
                if not first:
                    dve.wait_ge(m_out[j], c2 * 16)
                tt(amat[j][:, :], ps[:, j, :], avgm[:, :], ALU.add).then_inc(m_sb, 1)

            for j in range(2):
                mix_step(0, j, True)
            with dve.Fori(1, NCH // 2) as c2:
                for j in range(2):
                    mix_step(c2, j, False)

            pr3 = prob.rearrange("p h s m -> p (h s) m")

            def step(s, k):
                i0, i1, i2, i3, i4, i5, i6 = (Group(s, k - d) for d in range(7))

                def norm_sum(src, kk, d):
                    dve.tensor_reduce(lsum[kk], slots(src), AX.X, ALU.add).then_inc(d, 1)

                def norm_nd(src, g, kk, d, per):
                    need(dve, d, per, g, per - 1)
                    dve.scalar_tensor_tensor(slots(nd[kk]), per_slot(lsum[kk]), 1.0 / C, slots(src),
                                             ALU.mult, ALU.subtract).then_inc(d, 1)

                def norm_var(g, kk, sqd, ssd):
                    need(dve, sqd, 1, g, 1)
                    dve.tensor_reduce(lssq[kk], slots(nsq[kk]), AX.X, ALU.add).then_inc(ssd, 1)

                def norm_scale(g, kk, rtd, nn):
                    need(dve, rtd, 1, g, 1)
                    dve.reciprocal(lrs[kk], lrt[kk]).then_inc(nn, 1)
                    need(dve, nn, 2, g, 1)
                    tt(slots(nd[kk]), slots(nd[kk]), per_slot(lrs[kk]), ALU.mult).then_inc(nn, 1)

                def qkv_out(p):
                    need(dve, qkv_ps, 4, i0, p + 1)
                    if p == 0:
                        need(dve, qk_norm, 1, i1, 1)
                        need(dve, squared, 1, i1, 1)
                        need(dve, pv_ps, 1, i4, 1)
                    tt(qk[:, 2 * p:2 * p + 2, :],
                       mmb[p % 2][:, 0:6 * C].rearrange("p (s n) -> p s n", s=2)[:, :, 0:2 * C],
                       bqk.unsqueeze(1).to_broadcast([P, 2, 2 * C]), ALU.add).then_inc(qkv_sb, 1)
                    dve.tensor_copy(vpad[k][:, 2 * p:2 * p + 2, :, 0:HD],
                                    mmb[p % 2][:, 0:6 * C].rearrange("p (s n) -> p s n", s=2)[:, :, 2 * C:3 * C]
                                    .rearrange("p s (h d) -> p s h d", h=HEADS)).then_inc(v_put, 1)

                if there(i3):
                    need(dve, proj_ps, 1, i3, 1)
                    norm_sum(acc, 0, ln1_d)
                if there(i0):
                    qkv_out(0)
                if there(i3):
                    need(dve, x1_sb, 3, i4, 2)
                    norm_nd(acc, i3, 0, ln1_d, 2)
                if there(i0):
                    for p in (1, 2, 3):
                        qkv_out(p)
                if there(i3):
                    norm_var(i3, 0, ln1_sq, ln1_ss)
                if there(i0):
                    need(dve, squared, 1, i0, 1)
                    need(dve, rooted, 1, i1, 1)
                    dve.tensor_reduce(ss, sq.rearrange("p (n d) -> p n d", d=HD), AX.X, ALU.add).then_inc(summed, 1)
                    need(dve, summed, 2, i0, 1)
                    ts(ss, ss, 1e-24, None, ALU.max).then_inc(summed, 1)
                if there(i3):
                    norm_scale(i3, 0, ln1_rt, ln1_n)
                if there(i2):
                    need(dve, exped, 1, i2, 1)
                    dve.tensor_reduce(sm, pr3, AX.X, ALU.add).then_inc(prob_sum, 1)
                    need(dve, prob_sum, 2, i2, 1)
                    need(dve, probs, 1, i3, 1)
                    dve.reciprocal(rs, sm).then_inc(prob_sum, 1)
                if there(i0):
                    need(dve, rooted, 1, i0, 1)
                    need(dve, qk_norm, 1, i1, 1)
                    dve.reciprocal(rn, rt).then_inc(factor, 1)
                    need(dve, factor, 2, i0, 1)
                    rq = rn.rearrange("p (s k h) -> p s k h", s=SLOTS, k=2)[:, :, 0, :]
                    tt(rq, rq, scale.unsqueeze(1).to_broadcast([P, SLOTS, HEADS]), ALU.mult).then_inc(factor, 1)
                if there(i5):
                    norm_scale(i5, 1, ln2_rt, ln2_n)
                if there(i3):
                    need(dve, x1T_ps, 1, i3, 1)
                    dve.tensor_copy(x1T, tr).then_inc(x1T_sb, 1)
                if there(i2):
                    need(dve, probs, 1, i2, 1)
                    need(dve, pv_ps, 1, i3, 1)
                    dve.transpose(probT.rearrange("p h s n -> p (h s n)"),
                                  prob.rearrange("p h s m -> p (h s m)")).then_inc(probT_sb, 1)
                if there(i1):
                    need(dve, S_ps, 1, i1, 1)
                    need(dve, probT_sb, 1, i2, 1)
                    tt(prob, S, relb.unsqueeze(2).to_broadcast([P, HEADS, SLOTS, 32]), ALU.add).then_inc(biased, 1)
                if there(i4):
                    need(dve, fc2_ps, 1, i4, 1)
                    tt(slots(h2), slots(acc), row(b2), ALU.add).then_inc(ln2_d, 1)
                if there(i1):
                    need(dve, biased, 1, i1, 1)
                    need(dve, shifted, 1, i2, 1)
                    dve.tensor_reduce(mx, pr3, AX.X, ALU.max).then_inc(maxed, 1)
                if there(i4):
                    need(dve, ln2_d, 3, i4, 1)
                    norm_sum(h2, 1, ln2_d)
                    need(dve, y_sb, 2, i5, 2)
                    norm_nd(h2, i4, 1, ln2_d, 3)
                if there(i5):
                    need(dve, yT_ps, 1, i5, 1)
                    if k == 1 and not (isinstance(s, int) and s < 2):
                        dve.wait_ge(y_out, s * 32 - 32)
                    dve.tensor_copy(ystripe[:, :, (k - LAG) % GPS, :].rearrange("p r (i j) -> p i r j", j=CPS),
                                    tr.rearrange("p (i r j) -> p i r j", i=PAIRS, j=CPS)).then_inc(yT_sb, 1)
                if there(i4):
                    norm_var(i4, 1, ln2_sq, ln2_ss)

            over_groups(dve, step)

            def put(b, cq, j):
                dve.wait_ge(o_ps, cq * NB + (b * NCH + j + 1))
                dve.tensor_copy(orow[:, :, :, bass.ds(cq * NB + j, 1)].rearrange("p k n c -> p (k n) c"),
                                ps[:, j, :].unsqueeze(2)).then_inc(o_dve, 1)

            dve.wait_ge(y_out, 32 * NS)
            for b in range(BL1):
                if b:
                    dve.wait_ge(rows_out, 64 * b)
                with dve.Fori(0, NCH // NB) as cq:
                    for j in (1, 3):
                        put(b, cq, j)

        @block.gpsimd
        def _(pool):
            tt = pool.tensor_tensor
            pool.memset(ident, 0.0).then_inc(made_id, 1)
            pool.wait_ge(made_id, 1)
            pool.affine_select(out=ident, in_=ident, compare_op=ALU.not_equal, fill=1.0, base=0,
                               pattern=[[-1, P]], channel_multiplier=1).then_inc(made_id, 1)
            pool.memset(qkn, 0.0).then_inc(made_id, 1)
            for v in vpad:
                pool.memset(v, 0.0).then_inc(made_id, 1)
            pool.wait_ge(made_id, 7)
            for v in vpad:
                pool.memset(v[:, :, :, HD:HD + 1], 1.0).then_inc(made_id, 1)
            pool.wait_ge(made_id, 11)
            pool.wait_ge(consts, consts_in)
            pool.tensor_copy(pickb, ident).then_inc(pick_made, 1)
            pool.wait_ge(pick_made, 1)
            tt(pickb[:, HD:HD + 1], pickb[:, HD:HD + 1], bvcol, ALU.add).then_inc(made_id, 1)

            def step(s, k):
                i0, i1, i2, i3, i4, i5, i6 = (Group(s, k - d) for d in range(7))
                par = k % 2
                hs = HEADS * SLOTS
                pr3 = prob.rearrange("p h s m -> p (h s) m")
                if there(i3):
                    need(pool, ln1_n, 2, i3, 2)
                    need(pool, x1T_ps, 1, i4, 1)
                    tt(slots(nd[0]), slots(nd[0]), row(g1), ALU.mult).then_inc(x1_sb, 1)
                    need(pool, x1_sb, 3, i3, 1)
                    tt(x1, xo1[(k - 3) % 4], nd[0], ALU.subtract).then_inc(x1_sb, 1)
                if there(i2):
                    need(pool, prob_sum, 2, i2, 2)
                    tt(pr3, pr3, rs.unsqueeze(2).to_broadcast([P, hs, 32]), ALU.mult).then_inc(probs, 1)
                if there(i0):
                    need(pool, factor, 2, i0, 2)
                    need(pool, qkT_ps, 4, i1, 4)
                    tt(qkn.rearrange("p s k h d -> p (s k h) d")[:, :, 0:HD],
                       qk.rearrange("p s (n d) -> p (s n) d", d=HD),
                       rn.unsqueeze(2).to_broadcast([P, SLOTS * 2 * HEADS, HD]), ALU.mult).then_inc(qk_norm, 1)
                if there(i5):
                    need(pool, ln2_n, 2, i5, 2)
                    need(pool, yT_ps, 1, i6, 1)
                    tt(slots(nd[1]), slots(nd[1]), row(g2), ALU.mult).then_inc(y_sb, 1)
                    need(pool, y_sb, 2, i5, 1)
                    tt(yo, x1o2[(k - 5) % 2], nd[1], ALU.subtract).then_inc(y_sb, 1)
                if there(i1):
                    need(pool, maxed, 1, i1, 1)
                    tt(pr3, pr3, mx.unsqueeze(2).to_broadcast([P, hs, 32]), ALU.subtract).then_inc(shifted, 1)
                if there(i3):
                    need(pool, x1_sb, 3, i3, 2)
                    need(pool, y_sb, 2, i5, 2)
                    tt(slots(x1o2[(k - 3) % 2]), slots(x1), row(o2), ALU.add).then_inc(x1_sb, 1)
                if there(i0):
                    pool.wait_ge(x_in[par], s * (2 * SLOTS * 16) + (k // 2 + 1) * SLOTS * 16)
                    tt(slots(xo1[k]), xin[par], row(o1), ALU.add).then_inc(xo_put, 1)

            over_groups(pool, step)


def arrays_of(inputs):
    L0, L1 = "L0_conv_", "L1_conv_"
    t = lambda n: np.ascontiguousarray(np.asarray(inputs[L0 + n]).T)
    row = lambda n: np.asarray(inputs[L0 + n]).reshape(1, -1)
    cols = lambda n: np.ascontiguousarray(np.asarray(inputs[L0 + n]).reshape(-1, P).T)
    a = {"x": np.asarray(inputs["x"]), "qkv_wt": t("qkv_w"), "qkv_b": row("qkv_b"),
         "v_b": np.asarray(inputs[L0 + "qkv_b"])[2 * C:].reshape(-1, 1), "proj_wt": t("proj_w"),
         "proj_b": row("proj_b"), "logit_scale": np.asarray(inputs[L0 + "logit_scale"]).reshape(-1),
         "cpb_w1t": t("cpb_w1"), "cpb_b1": cols("cpb_b1"), "cpb_w2t": t("cpb_w2"),
         "n1g": row("norm1_g"), "n1b": row("norm1_b"), "n2g": row("norm2_g"), "n2b": row("norm2_b"),
         "fc1_wt": t("fc1_w"), "fc1_b": cols("fc1_b"), "fc2_wt": t("fc2_w"), "fc2_b": row("fc2_b"),
         "w_real": np.asarray(inputs[L1 + "w_real"]), "w_imag": np.asarray(inputs[L1 + "w_imag"])}
    a.update(shape_constants())
    return a


def kernel(**inputs):
    import concourse.bacc as _bacc
    from concourse.bass_utils import run_bass_kernel_spmd as _run

    nc = _bacc.Bacc("TRN2", target_bir_lowering=False, num_devices=1)
    arrays, args = {}, []
    for name, a in arrays_of(inputs).items():
        arrays[f"in_{name}"] = a
        args.append(nc.dram_tensor(f"in_{name}", a.shape, F32, kind="ExternalInput").ap())
    shape = tuple(inputs["x"].shape)
    args.append(nc.dram_tensor("out", shape, F32, kind="ExternalOutput").ap())
    b, h, w, c = shape
    args.append(nc.dram_tensor("y", (b, h, c, w), F32, kind="Internal").ap())
    args.append(nc.dram_tensor("mix", (C, P, 2 * T), F32, kind="Internal").ap())
    swin_then_fourier(nc, *args)
    r = _run(nc, [arrays], core_ids=[0])
    return r.results[0]["out"]
```

```python
from collections import namedtuple
from contextlib import ExitStack

import numpy as np
import concourse.bass as bass
from concourse import mybir

F32 = mybir.dt.float32
ALU = mybir.AluOpType
ACT = mybir.ActivationFunctionType
AX = mybir.AxisListType

P = 128
C = 64
HEADS, HD = 4, 16
WIN = 4
HID = 256
ROWS = 16
CPS = 8
SLOTS = 8
PAIRS = SLOTS // 2
GPS = 4
LAG = 6
PEEL = 2
OFF = -30000.0
RELS = (2 * WIN - 1) ** 2
KERNEL = 25
MODES = 128
T = 256

Group = namedtuple("Group", "s off")


def shape_constants():
    ax = np.arange(-(WIN - 1), WIN, dtype=np.float32)
    t = np.stack(np.meshgrid(ax, ax, indexing="ij"), axis=-1)
    t /= WIN - 1
    t *= 8.0
    t = np.sign(t) * np.log2(np.abs(t) + 1.0) / 3.0
    coords = np.ascontiguousarray(t.reshape(-1, 2).astype(np.float32).T)
    pick = np.zeros((RELS + 1, 32, P), np.float32)
    for p in range(P):
        qi, qj = (p % 32) // CPS, p % CPS
        for m in range(32):
            ki, kj = m // CPS, m % CPS
            if qj // WIN == kj // WIN:
                pick[(qi - ki + WIN - 1) * (2 * WIN - 1) + (qj - kj + WIN - 1), m, p] = 1
            else:
                pick[RELS, m, p] = 1
    ma = np.zeros((T, T))
    for i in range(T):
        for j in range(i - KERNEL // 2, i + KERNEL // 2 + 1):
            ma[i, min(max(j, 0), T - 1)] += 1.0 / KERNEL
    s, m = np.arange(T), np.arange(MODES)
    ang = 2 * np.pi * ((m[:, None] * s[None, :]) % T) / T
    season = np.eye(T) - ma
    fr, fi = np.cos(ang) @ season, -np.sin(ang) @ season
    amp = np.where(m == 0, 1.0, 2.0)[:, None] / T
    cr, ci = amp * np.cos(ang), -amp * np.sin(ang)
    dft = np.concatenate([fr, fi, -fi, fr], axis=1)
    inverse = np.concatenate([cr, ci], axis=1)
    average = np.concatenate([ma.T[:P], ma.T[P:]], axis=1)
    return {"coords": coords, "pick": pick.reshape(RELS + 1, 32 * P),
            "dft": dft.astype(np.float32), "inverse": inverse.astype(np.float32),
            "average": average.astype(np.float32)}


def swin_then_fourier(nc, x, qkv_wt, qkv_b, v_b, proj_wt, proj_b, logit_scale, cpb_w1t, cpb_b1, cpb_w2t,
                      n1g, n1b, n2g, n2b, fc1_wt, fc1_b, fc2_wt, fc2_b, w_real, w_imag,
                      coords, pick, dft, inverse, average, out, y, mix):
    B, H, W, _ = x.shape
    NS = B * H // ROWS
    G = NS * GPS
    BL1, NCH = out.shape[0], C
    HALF = W // 2
    GC = HALF // GPS
    xr = x.rearrange("b h w c -> (b h) w c")
    yr = y.rearrange("b h c w -> (b h) c w")

    with ExitStack() as ctx:
        def sb(name, cols):
            return ctx.enter_context(nc.sbuf_tensor(name, [P, cols], F32))

        def sem(name):
            return ctx.enter_context(nc.semaphore(name))

        ps = ctx.enter_context(nc.psum_tensor("ps", [P, 8, 512], F32))
        arena = sb("arena", 2 * T * C)
        used = [0]

        def carve(cols):
            a = used[0]
            used[0] += cols
            assert used[0] <= 2 * T * C
            return arena[:, a:a + cols]

        ident = carve(P)
        wqkv = carve(2 * 3 * C).rearrange("p (a n) -> p a n", a=2)
        wproj = carve(C)
        w1 = carve(2 * HID).rearrange("p (a n) -> p a n", a=2)
        b1 = carve(2)
        w2 = carve(2 * C).rearrange("p (k n) -> p k n", k=2)
        bqk = carve(2 * C)
        bvcol, pickb, wproj2 = carve(1), carve(P), carve(C)
        g1, o1, g2, o2 = (carve(C) for _ in range(4))
        b2 = carve(1)
        scale = carve(HEADS)
        eps, warm = carve(1), carve(3)
        relb = carve(HEADS * 32).rearrange("p (h m) -> p h m", h=HEADS)
        picks = carve(32 * P).rearrange("p (m q) -> p m q", m=32)
        cw1, cco = carve(512), carve(RELS)
        cb1 = carve(4)
        cw2 = carve(4 * HEADS).rearrange("p (k h) -> p k h", k=4)
        hid = carve(4 * RELS).rearrange("p (k r) -> p k r", k=4)
        table = carve(HEADS)
        SC = SLOTS * C
        xin = [carve(SC).rearrange("p (s c) -> p s c", s=SLOTS) for _ in range(2)]
        xo1 = [carve(SC) for _ in range(4)]
        xT = carve(PAIRS * P).rearrange("p (s n) -> p s n", s=PAIRS)
        qk = carve(SLOTS * 2 * C).rearrange("p (s n) -> p s n", s=SLOTS)
        sq = carve(SLOTS * 2 * C)
        ss, rt, rn = (carve(SLOTS * 2 * HEADS) for _ in range(3))
        qkn = carve(SLOTS * 2 * P).rearrange("p (s k h d) -> p s k h d", s=SLOTS, k=2, h=HEADS)
        qkT = carve(SLOTS * 2 * P).rearrange("p (s k n) -> p s k n", s=SLOTS, k=2)
        vpad = [sb(f"vpad{i}", SLOTS * P)[:, :].rearrange("p (s h d) -> p s h d", s=SLOTS, h=HEADS)
                for i in range(4)]
        prob = carve(HEADS * SLOTS * 32).rearrange("p (h s m) -> p h s m", h=HEADS, s=SLOTS)
        mx, sm, rs = (carve(HEADS * SLOTS) for _ in range(3))
        probT = carve(HEADS * SLOTS * 32).rearrange("p (h s n) -> p h s n", h=HEADS, s=SLOTS)
        oT = carve(SLOTS * P).rearrange("p (s g n) -> p s g n", s=SLOTS, g=4)
        nd, nsq = [carve(SC) for _ in range(2)], [carve(SC) for _ in range(2)]
        lsum, lssq, lrt, lrs = ([carve(SLOTS) for _ in range(2)] for _ in range(4))
        x1 = [carve(SC) for _ in range(2)]
        x1o2 = [carve(SC) for _ in range(4)]
        x1T = carve(PAIRS * P)
        hT = carve(2 * 2 * 512).rearrange("p (a k n) -> p a k n", a=2, k=2)
        hcT = carve(PAIRS * P)
        yo = carve(SC)
        ystripe = carve(ROWS * HALF).rearrange("p (r q n) -> p r q n", r=ROWS, q=GPS)
        NB = 4
        dftm, invm, avgm = sb("dftm", 1024), sb("invm", 512), sb("avgm", 512)
        wri = [sb(f"wri{i}", 2 * P) for i in range(2)]
        vri = [sb(f"vri{i}", 512) for i in range(2)]
        amat = [sb(f"amat{i}", 512) for i in range(NB)]
        xch = [sb(f"xch{i}", 512) for i in range(NB)]
        orow = arena[:, :].rearrange("p (k n c) -> p k n c", k=2, c=C)

        att = ps[:, 0:4, :]
        S = att[:, :, 0:256].rearrange("p h (s m) -> p h s m", m=32)
        PV = att[:, :, 256:512].rearrange("p g (s n) -> p g s n", n=32)
        mmb = [ps[:, 4, :], ps[:, 5, :]]
        acc, tr = ps[:, 6, :], ps[:, 7, :]

        consts, made, set_up = sem("consts"), sem("made"), sem("set_up")
        made_id, pick_made = sem("made_id"), sem("pick_made")
        x_in = [sem("x_in0"), sem("x_in1")]
        xT_ps, xT_sb = sem("xT_ps"), sem("xT_sb")
        qkv_ps, qkv_sb = sem("qkv_ps"), sem("qkv_sb")
        squared, summed = sem("squared"), sem("summed")
        rooted, factor = sem("rooted"), sem("factor")
        qk_norm, v_put, xo_put = sem("qk_norm"), sem("v_put"), sem("xo_put")
        qkT_ps, qkT_sb = sem("qkT_ps"), sem("qkT_sb")
        S_ps, biased, maxed, shifted = sem("S_ps"), sem("biased"), sem("maxed"), sem("shifted")
        exped, prob_sum, probs, probT_sb = sem("exped"), sem("prob_sum"), sem("probs"), sem("probT_sb")
        pv_ps, oT_sb, proj_ps = sem("pv_ps"), sem("oT_sb"), sem("proj_ps")
        ln1_d, ln1_sq, ln1_ss, ln1_rt, ln1_n = (sem(f"ln1_{n}") for n in ("d", "sq", "ss", "rt", "n"))
        ln2_d, ln2_sq, ln2_ss, ln2_rt, ln2_n = (sem(f"ln2_{n}") for n in ("d", "sq", "ss", "rt", "n"))
        x1_sb, x1T_ps, x1T_sb = sem("x1_sb"), sem("x1T_ps"), sem("x1T_sb")
        fc1_ps, gelued, fc2_ps = sem("fc1_ps"), sem("gelued"), sem("fc2_ps")
        h_sb, h_ps = sem("h_sb"), sem("h_ps")
        y_sb, yT_ps, yT_sb, y_out = sem("y_sb"), sem("yT_ps"), sem("yT_sb"), sem("y_out")
        w_in = [sem("w_in0"), sem("w_in1")]
        v_ps, v_sb, m_ps, m_sb = sem("v_ps"), sem("v_sb"), sem("m_ps"), sem("m_sb")
        m_out = [sem(f"m_out{i}") for i in range(NB)]
        ch_in = [sem(f"ch_in{i}") for i in range(NB)]
        o_ps, o_act, o_dve, rows_out = sem("o_ps"), sem("o_act"), sem("o_dve"), sem("rows_out")

        def there(g):
            return not isinstance(g.s, int) or 0 <= g.s * GPS + g.off < G

        def need(eng, s, per, g, n):
            if there(g):
                eng.wait_ge(s, g.s * (GPS * per) + (g.off * per + n))

        def over_groups(eng, step):
            for i in range(PEEL * GPS):
                step(i // GPS, i % GPS)
            with eng.Fori(PEEL, NS) as s:
                for k in range(GPS):
                    step(s, k)
            for i in range(LAG):
                step(NS + i // GPS, i % GPS)

        last = Group(NS - 1, GPS - 1)

        def row(t):
            return t.unsqueeze(1).to_broadcast([P, SLOTS, C])

        def slots(t):
            return t.rearrange("p (s c) -> p s c", s=SLOTS)

        def per_slot(t):
            return t.unsqueeze(2).to_broadcast([P, SLOTS, C])

        consts_in = 16 * 31
        block = ctx.enter_context(nc.Block())

        @block.sync
        def _(sp):
            n = [0]

            def const(dst, src):
                n[0] += 1
                sp.dma_start(dst, src).then_inc(consts, 16)

            sp.wait_ge(set_up, 7)
            for a in range(2):
                const(wqkv[a * C:a * C + C, a, :], qkv_wt)
                const(w1[a * C:a * C + C, a, :], fc1_wt)
            for h in range(HEADS):
                const(wproj[32 * h:32 * h + HD, :], proj_wt[h * HD:h * HD + HD, :])
            const(wproj[HD:HD + 1, :], proj_b)
            const(b1, fc1_b)
            const(w2, fc2_wt.rearrange("(k p) n -> p k n", k=2))
            const(scale, logit_scale.partition_broadcast(P))
            const(bqk[:, 0:C], qkv_b[0, 0:C].partition_broadcast(P))
            for h in range(HEADS):
                const(bvcol[32 * h:32 * h + HD, :], v_b[h * HD:h * HD + HD, :])
            for dst, src in ((g1, n1g), (o1, n1b), (g2, n2g), (o2, n2b)):
                const(dst, src[0, :].partition_broadcast(P))
            for a in range(2):
                const(b2[a * C:a * C + C, :], fc2_b)
            const(picks[0:RELS + 1], pick.rearrange("r (m q) -> r m q", m=32))
            const(cw1[0:2, :], cpb_w1t)
            const(cco[0:2, :], coords)
            const(cb1, cpb_b1)
            const(cw2, cpb_w2t.rearrange("(k p) h -> p k h", k=4))
            const(dftm[:, :], dft)
            const(invm[:, :], inverse)
            const(avgm[:, :], average)
            assert 16 * n[0] == consts_in

            def mix_loads(c2, j, first):
                if not first:
                    sp.wait_ge(v_ps, c2 * 2 + (j - 1))
                sp.dma_start(wri[j][:, 0:P], w_real[bass.ds(c2 * 2 + j, 1)].rearrange("a m k -> (a m) k")).then_inc(w_in[j], 16)
                sp.dma_start(wri[j][:, P:2 * P], w_imag[bass.ds(c2 * 2 + j, 1)].rearrange("a m k -> (a m) k")).then_inc(w_in[j], 16)

            def mix_store(c2, j):
                sp.wait_ge(m_sb, c2 * 2 + j + 1)
                sp.dma_start(mix[bass.ds(c2 * 2 + j, 1)].rearrange("a p n -> (a p) n"), amat[j][:, :]).then_inc(m_out[j], 16)

            mix_loads(0, 0, True)
            mix_loads(0, 1, True)
            with sp.Fori(1, NCH // 2) as c2:
                for j in range(2):
                    mix_loads(c2, j, False)
                for j in range(2):
                    mix_store(c2 - 1, j)
            for j in range(2):
                mix_store(NCH // 2 - 1, j)

            def load_x(g):
                par = g.off % 2
                q = g.off % GPS
                need(sp, xT_ps, 1, Group(g.s, g.off - 2), 1)
                need(sp, xo_put, 1, Group(g.s, g.off - 2), 1)
                src = xr[bass.ds(g.s * ROWS, ROWS)] if g.off < GPS else xr[bass.ds((g.s + 1) * ROWS, ROWS)]
                for sl in range(SLOTS):
                    c0 = (sl % 2) * HALF + q * GC + (sl // 2) * CPS
                    sp.dma_start(xin[par][:, sl, :], src[:, c0:c0 + CPS, :]).then_inc(x_in[par], 16)

            def store_y(s):
                need(sp, yT_sb, 1, Group(s, GPS - 1), 1)
                for a in range(2):
                    sp.dma_start(
                        yr[bass.ds(s * ROWS, ROWS), :, a * HALF:(a + 1) * HALF].rearrange("r c n -> c r n"),
                        ystripe[a * C:(a + 1) * C].rearrange("p r q n -> p r (q n)")).then_inc(y_out, 16)

            load_x(Group(0, 0))
            load_x(Group(0, 1))

            def step(s, k):
                if k < 2 or not isinstance(s, int) or s < NS - 1:
                    if there(Group(s, k + 2)):
                        load_x(Group(s, k + 2))
                if k == 1 and not (isinstance(s, int) and s < 2):
                    store_y(s - 2)

            for i in range(PEEL * GPS):
                step(i // GPS, i % GPS)
            with sp.Fori(PEEL, NS - 1) as s:
                for k in range(GPS):
                    step(s, k)
            for i in range(GPS + LAG):
                step(NS - 1 + i // GPS, i % GPS)
            sp.wait_ge(y_out, 32 * NS)
            for j in range(2):
                sp.wait_ge(m_out[j], 16 * (NCH // 2))

            def channel_in(b, cq, j, before):
                if before is not None:
                    sp.wait_ge(o_ps, before)
                c = cq * NB + j
                sp.dma_start(amat[j][:, :], mix[bass.ds(c, 1)].rearrange("a p n -> (a p) n")).then_inc(ch_in[j], 16)
                sp.dma_start(xch[j][:, :].rearrange("p (k n) -> p k n", k=2),
                             y[b].rearrange("(k t) c n -> t k c n", k=2)[:, :, bass.ds(c, 1), :].rearrange("t k c n -> t k (c n)")).then_inc(ch_in[j], 16)

            for b in range(BL1):
                for j in range(NB):
                    channel_in(b, 0, j, b * NCH + j + 1 - NB if b else None)
                with sp.Fori(1, NCH // NB) as cq:
                    for j in range(NB):
                        channel_in(b, cq, j, cq * NB + (b * NCH + j + 1 - NB))

        @block.tensor
        def _(pe):
            mm = pe.matmul
            pe.wait_ge(consts, consts_in)
            for k in range(4):
                mm(acc[:, k * RELS:(k + 1) * RELS], cw1[0:2, k * P:(k + 1) * P], cco[0:2, :],
                   start=True, stop=True).then_inc(made, 1)
            pe.wait_ge(set_up, 8)
            for k in range(4):
                ins = mm(tr[0:RELS, 0:HEADS], hid[:, k, :], cw2[:, k, :], start=(k == 0), stop=(k == 3))
            ins.then_inc(made, 1)
            pe.wait_ge(set_up, 10)
            for m in range(32):
                ins = mm(acc.rearrange("p (m h) -> p m h", h=HEADS)[:, m, :], picks[0:RELS + 1, m, :],
                         table[0:RELS + 1, :], start=True, stop=True)
            ins.then_inc(made, 1)
            pe.wait_ge(made_id, 12)
            mm(tr[:, 0:C], pickb, wproj, start=True, stop=True).then_inc(made, 1)

            def mix_step(c2, j, first):
                pe.wait_ge(w_in[j], c2 * 32 + 32)
                if not first:
                    pe.wait_ge(v_sb, c2 * 2 + (j - 1))
                mm(mmb[j], wri[j][:, 0:P], dftm[:, 0:512], start=True, stop=False)
                mm(mmb[j], wri[j][:, P:2 * P], dftm[:, 512:1024], start=False, stop=True).then_inc(v_ps, 1)

            def mix_step2(c2, j, first):
                pe.wait_ge(v_sb, c2 * 2 + j + 1)
                if not first:
                    pe.wait_ge(m_sb, c2 * 2 + (j - 1))
                for k in range(2):
                    for r in range(2):
                        ins = mm(ps[:, j, k * T:(k + 1) * T], vri[j][:, r * T + k * P:r * T + (k + 1) * P],
                                 invm[:, r * T:(r + 1) * T], start=(r == 0), stop=(r == 1))
                ins.then_inc(m_ps, 1)

            for j in range(2):
                mix_step(0, j, True)
            for j in range(2):
                mix_step2(0, j, True)
            with pe.Fori(1, NCH // 2) as c2:
                for j in range(2):
                    mix_step(c2, j, False)
                for j in range(2):
                    mix_step2(c2, j, False)
            pe.wait_ge(m_sb, NCH)
            pe.wait_ge(set_up, 14)
            pe.wait_ge(made_id, 11)

            def step(s, k):
                i0, i1, i2, i3, i4, i5, i6, i7 = (Group(s, k - d) for d in range(8))
                par = k % 2

                def turn(dst, tiles, done):
                    for j, t in enumerate(tiles):
                        ins = pe.transpose(dst[:, j * P:(j + 1) * P], t, ident)
                    ins.then_inc(done, 1)

                def scores(sl):
                    for h in range(HEADS):
                        for g in range(4):
                            ins = mm(S[32 * g:32 * g + 32, h, sl, :],
                                     qkT[32 * h:32 * h + HD, sl, 0, 32 * g:32 * g + 32],
                                     qkT[32 * h:32 * h + HD, sl, 1, 32 * g:32 * g + 32],
                                     start=True, stop=True, tile_position=(32 * h, 32 * g))
                    if sl == SLOTS - 1:
                        ins.then_inc(S_ps, 1)

                def weighted(sl):
                    for g in range(4):
                        for h in range(HEADS):
                            ins = mm(PV[32 * h:32 * h + 32, g, sl, :], vpad[(k - 2) % 4][32 * g:32 * g + 32, sl, h, :],
                                     probT[32 * g:32 * g + 32, h, sl, :], start=True, stop=True,
                                     tile_position=(32 * g, 32 * h))
                    if sl == SLOTS - 1:
                        ins.then_inc(pv_ps, 1)

                def second_layer(kk):
                    if kk == 0:
                        need(pe, gelued, 4, i5, 4)
                        need(pe, ln1_d, 2, i3, 2)
                        if not there(i3):
                            need(pe, ln2_d, 2, i6, 2)
                    for a in range(2):
                        ins = mm(acc[a * C:a * C + C, :], w2[:, kk, :], hT[:, a, kk, :],
                                 start=(kk == 0), stop=(kk == 1), tile_position=(0, a * C))
                    if kk == 1:
                        ins.then_inc(fc2_ps, 1)

                def qk_turned(f):
                    if f == 0:
                        need(pe, qk_norm, 1, i1, 1)
                    if f < 2:
                        need(pe, gelued, 4, i5, 3 + f)
                        if not there(i5):
                            need(pe, v_put, 4, i1, 3 + f)
                    else:
                        need(pe, qkT_sb, 4, i1, f - 1)
                    turn(mmb[f % 2], [qkn[:, 2 * f + j // 2, j % 2, :, :].rearrange("p h d -> p (h d)")
                                      for j in range(4)], qkT_ps)

                def project(p):
                    if p == 0:
                        need(pe, oT_sb, 1, i3, 1)
                        need(pe, ln2_d, 2, i6, 2)
                        if not there(i6):
                            need(pe, ln1_d, 2, i4, 2)
                    for sl in (2 * p, 2 * p + 1):
                        ins = mm(acc[:, sl * C:(sl + 1) * C], oT[:, sl, :, :].rearrange("p g n -> p (g n)"),
                                 wproj2, start=True, stop=True)
                    if p == PAIRS - 1:
                        ins.then_inc(proj_ps, 1)

                def qkv(p):
                    if p == 0:
                        need(pe, xT_sb, 1, i0, 1)
                    if p < 2:
                        need(pe, qkT_sb, 4, i1, 3 + p)
                    else:
                        need(pe, v_put, 4, i0, p - 1)
                    mm(mmb[p % 2][:, 0:6 * C], xT[:, p, :], wqkv.rearrange("p a n -> p (a n)"),
                       start=True, stop=True).then_inc(qkv_ps, 1)

                def first_layer(j):
                    if j == 0:
                        need(pe, x1T_sb, 1, i4, 1)
                    if j < 2:
                        need(pe, v_put, 4, i0, 3 + j)
                        if not there(i0):
                            need(pe, qkT_sb, 4, i1, 3 + j)
                            need(pe, gelued, 4, i5, 3 + j)
                    else:
                        need(pe, gelued, 4, i4, j - 1)
                    mm(mmb[j % 2], w1[:, j // 2, (j % 2) * P:(j % 2 + 1) * P], x1T,
                       start=True, stop=True).then_inc(fc1_ps, 1)

                if there(i0):
                    pe.wait_ge(x_in[par], s * (2 * SLOTS * 16) + (k // 2 + 1) * SLOTS * 16)
                    need(pe, yT_sb, 1, i7, 1)
                    if not there(i7):
                        need(pe, x1T_sb, 1, i5, 1)
                        need(pe, xT_sb, 1, i1, 1)
                    turn(tr, [xin[par][:, 2 * p:2 * p + 2, :].rearrange("p s c -> p (s c)")
                              for p in range(PAIRS)], xT_ps)
                if there(i1):
                    qk_turned(0)
                    qk_turned(1)
                if there(i3):
                    project(0)
                    project(1)
                if there(i1):
                    qk_turned(2)
                if there(i3):
                    project(2)
                if there(i1):
                    qk_turned(3)
                if there(i3):
                    project(3)
                if there(i0):
                    qkv(0)
                if there(i1):
                    need(pe, qkT_sb, 4, i1, 4)
                    need(pe, oT_sb, 1, i3, 1)
                    if not there(i3):
                        need(pe, biased, 1, i2, 1)
                if there(i0):
                    qkv(1)
                if there(i1):
                    scores(0)
                    scores(1)
                if there(i0):
                    qkv(2)
                    qkv(3)
                if there(i1):
                    scores(2)
                    scores(3)
                if there(i4):
                    need(pe, x1_sb, 3, i4, 2)
                    need(pe, xT_sb, 1, i0, 1)
                    if not there(i0):
                        need(pe, yT_sb, 1, i7, 1)
                    turn(tr, [x1[k % 2][:, q * P:(q + 1) * P] for q in range(PAIRS)], x1T_ps)
                if there(i5):
                    second_layer(0)
                if there(i1):
                    scores(4)
                    scores(5)
                if there(i5):
                    second_layer(1)
                if there(i1):
                    scores(6)
                    scores(7)
                if there(i4):
                    first_layer(0)
                    first_layer(1)
                if there(i2):
                    need(pe, biased, 1, i1, 1)
                    need(pe, probT_sb, 1, i2, 1)
                    need(pe, v_put, 4, i2, 4)
                for p in range(PAIRS):
                    if p < 2 and there(i5):
                        if p == 0:
                            need(pe, h_sb, 1, i5, 1)
                        for q in (2 * p, 2 * p + 1):
                            ins = pe.transpose(acc[:, q * P:(q + 1) * P], hcT[:, q * P:(q + 1) * P], ident)
                        if p == 1:
                            ins.then_inc(h_ps, 1)
                    if p >= 2 and there(i4):
                        first_layer(p)
                    if p == 3 and there(i6):
                        need(pe, y_sb, 2, i6, 2)
                        need(pe, x1T_sb, 1, i4, 1)
                        if not there(i4):
                            need(pe, yT_sb, 1, i7, 1)
                        turn(tr, [yo[:, q * P:(q + 1) * P] for q in range(PAIRS)], yT_ps)
                    if there(i2):
                        weighted(2 * p)
                        weighted(2 * p + 1)

            over_groups(pe, step)

            def channel(b, cq, j, first):
                pe.wait_ge(ch_in[j], cq * 32 + (b * (NCH // NB) + 1) * 32)
                if not first:
                    pe.wait_ge(o_dve if j % 2 else o_act, cq * 2 + (b * (NCH // 2) + j // 2 - 1))
                for k in range(2):
                    for r in range(2):
                        ins = mm(ps[:, j, k * T:(k + 1) * T], amat[j][:, r * T + k * P:r * T + (k + 1) * P],
                                 xch[j][:, r * T:(r + 1) * T], start=(r == 0), stop=(r == 1))
                ins.then_inc(o_ps, 1)

            for b in range(BL1):
                for j in range(NB):
                    channel(b, 0, j, b == 0)
                with pe.Fori(1, NCH // NB) as cq:
                    for j in range(NB):
                        channel(b, cq, j, False)

        @block.scalar
        def _(act):
            f = act.activation
            act.wait_ge(consts, consts_in)
            act.wait_ge(set_up, 9)
            f(table[0:RELS, :], table[0:RELS, :], ACT.Sigmoid).then_inc(set_up, 1)
            act.wait_ge(set_up, 12)
            f(scale, scale, ACT.Exp).then_inc(set_up, 1)

            def mix_step(c2, j, first):
                act.wait_ge(v_ps, c2 * 2 + j + 1)
                if not first:
                    act.wait_ge(m_ps, c2 * 2 + (j - 1))
                f(vri[j][:, :], mmb[j], ACT.Copy).then_inc(v_sb, 1)

            for j in range(2):
                mix_step(0, j, True)
            with act.Fori(1, NCH // 2) as c2:
                for j in range(2):
                    mix_step(c2, j, False)

            def step(s, k):
                i0, i1, i2, i3, i4, i5, i6, i7 = (Group(s, k - d) for d in range(8))
                par = k % 2

                def norm_square(g, kk, d, sqd, ssd, last, prev):
                    need(act, d, last, g, last)
                    need(act, ssd, 1, prev, 1)
                    f(nsq[kk], nd[kk], ACT.Square).then_inc(sqd, 1)

                def norm_root(g, kk, ssd, rtd, nn, prev):
                    need(act, ssd, 1, g, 1)
                    need(act, nn, 2, prev, 2)
                    f(lrt[kk], lssq[kk], ACT.Sqrt, scale=1.0 / C, bias=eps).then_inc(rtd, 1)

                def load_table(i, func):
                    f(warm[:, i:i + 1], eps, func)

                if there(i3):
                    need(act, pv_ps, 1, i3, 1)
                    need(act, proj_ps, 1, i4, 1)
                    f(oT.rearrange("p s g n -> p g s n"), PV, ACT.Copy).then_inc(oT_sb, 1)
                if there(i0):
                    need(act, xT_ps, 1, i0, 1)
                    f(xT.rearrange("p s n -> p (s n)"), tr, ACT.Copy).then_inc(xT_sb, 1)
                if there(i1):
                    for j in range(4):
                        need(act, qkT_ps, 4, i1, j + 1)
                        if j == 0:
                            need(act, S_ps, 1, i2, 1)
                        f(qkT[:, 2 * j:2 * j + 2, :, :].rearrange("p s k n -> p (s k n)"), mmb[j % 2],
                          ACT.Copy).then_inc(qkT_sb, 1)
                if there(i2):
                    need(act, shifted, 1, i2, 1)
                    pr = prob.rearrange("p h s m -> p (h s m)")
                    f(pr, pr, ACT.Exp).then_inc(exped, 1)
                if there(i3):
                    norm_square(i3, 0, ln1_d, ln1_sq, ln1_ss, 2, i4)
                if there(i6):
                    norm_square(i6, 1, ln2_d, ln2_sq, ln2_ss, 2, i7)
                load_table(1, ACT.Sqrt)
                if there(i0):
                    need(act, qkv_sb, 4, i0, 4)
                    need(act, summed, 2, i1, 1)
                    f(sq, qk.rearrange("p s n -> p (s n)"), ACT.Square).then_inc(squared, 1)
                if there(i6):
                    norm_root(i6, 1, ln2_ss, ln2_rt, ln2_n, i7)
                if there(i3):
                    norm_root(i3, 0, ln1_ss, ln1_rt, ln1_n, i4)
                if there(i4):
                    need(act, x1T_ps, 1, i4, 1)
                    f(x1T, tr, ACT.Copy).then_inc(x1T_sb, 1)
                if there(i5):
                    need(act, fc2_ps, 1, i5, 1)
                    f(hcT, acc, ACT.Identity, bias=b2).then_inc(h_sb, 1)
                if there(i0):
                    need(act, summed, 2, i0, 2)
                    need(act, factor, 2, i1, 1)
                    f(rt, ss, ACT.Sqrt).then_inc(rooted, 1)
                if there(i4):
                    load_table(2, ACT.Gelu)
                    for j in range(4):
                        need(act, fc1_ps, 4, i4, j + 1)
                        if j == 0:
                            need(act, fc2_ps, 1, i5, 1)
                        f(hT[:, j // 2, j % 2, :], mmb[j % 2], ACT.Gelu, bias=b1[:, j % 2:j % 2 + 1]).then_inc(gelued, 1)
                if there(i1):
                    load_table(0, ACT.Exp)

            over_groups(act, step)

            def put(b, cq, j):
                act.wait_ge(o_ps, cq * NB + (b * NCH + j + 1))
                f(orow[:, :, :, bass.ds(cq * NB + j, 1)].rearrange("p k n c -> p (k n) c"),
                  ps[:, j, :].unsqueeze(2), ACT.Copy).then_inc(o_act, 1)

            act.wait_ge(y_out, 32 * NS)
            for b in range(BL1):
                if b:
                    act.wait_ge(rows_out, 64 * b)
                with act.Fori(0, NCH // NB) as cq:
                    for j in (0, 2):
                        put(b, cq, j)
                act.wait_ge(o_dve, (b + 1) * NCH // 2)
                act.wait_ge(o_act, (b + 1) * NCH // 2)
                for k in range(2):
                    for hh in range(2):
                        act.dma_start(out[b, k * P:(k + 1) * P, hh * 128:(hh + 1) * 128, :].rearrange("t n c -> t (n c)"),
                                      orow[:, k, hh * 128:(hh + 1) * 128, :].rearrange("p n c -> p (n c)"))\
                            .then_inc(rows_out, 16)
            act.wait_ge(rows_out, 64 * BL1)

        @block.vector
        def _(dve):
            tt, ts = dve.tensor_tensor, dve.tensor_scalar
            dve.memset(wqkv, 0.0).then_inc(set_up, 1)
            dve.memset(wproj, 0.0).then_inc(set_up, 1)
            dve.memset(w1, 0.0).then_inc(set_up, 1)
            dve.memset(bqk, 0.0).then_inc(set_up, 1)
            dve.memset(bvcol, 0.0).then_inc(set_up, 1)
            dve.memset(table, OFF / 16).then_inc(set_up, 1)
            dve.memset(eps, 1e-5).then_inc(set_up, 1)
            dve.wait_ge(consts, consts_in)
            dve.wait_ge(made, 4)
            for k in range(4):
                ins = ts(hid[:, k, :], acc[:, k * RELS:(k + 1) * RELS], cb1[:, k:k + 1], 0.0, ALU.add, ALU.max)
            ins.then_inc(set_up, 1)
            dve.wait_ge(made, 5)
            dve.wait_ge(set_up, 8)
            dve.tensor_copy(table[0:RELS, :], tr[0:RELS, 0:HEADS]).then_inc(set_up, 1)
            dve.wait_ge(made, 6)
            ts(relb.rearrange("p h m -> p m h"), acc[:, 0:P].rearrange("p (m h) -> p m h", h=HEADS),
               16.0, None, ALU.mult).then_inc(set_up, 1)
            dve.wait_ge(set_up, 11)
            ts(scale, scale, float(np.float32(np.log(100.0))), None, ALU.min).then_inc(set_up, 1)
            dve.wait_ge(set_up, 13)
            dve.wait_ge(made, 7)
            dve.tensor_copy(wproj2, tr[:, 0:C]).then_inc(set_up, 1)

            def mix_step(c2, j, first):
                dve.wait_ge(m_ps, c2 * 2 + j + 1)
                if not first:
                    dve.wait_ge(m_out[j], c2 * 16)
                tt(amat[j][:, :], ps[:, j, :], avgm[:, :], ALU.add).then_inc(m_sb, 1)

            for j in range(2):
                mix_step(0, j, True)
            with dve.Fori(1, NCH // 2) as c2:
                for j in range(2):
                    mix_step(c2, j, False)

            pr3 = prob.rearrange("p h s m -> p (h s) m")

            def step(s, k):
                i0, i1, i2, i3, i4, i5, i6, i7 = (Group(s, k - d) for d in range(8))

                def norm_sum(src, kk, d):
                    dve.tensor_reduce(lsum[kk], slots(src), AX.X, ALU.add).then_inc(d, 1)

                def norm_nd(src, g, kk, d):
                    need(dve, d, 2, g, 1)
                    dve.scalar_tensor_tensor(slots(nd[kk]), per_slot(lsum[kk]), 1.0 / C, slots(src),
                                             ALU.mult, ALU.subtract).then_inc(d, 1)

                def norm_var(g, kk, sqd, ssd):
                    need(dve, sqd, 1, g, 1)
                    dve.tensor_reduce(lssq[kk], slots(nsq[kk]), AX.X, ALU.add).then_inc(ssd, 1)

                def norm_scale(g, kk, rtd, nn):
                    need(dve, rtd, 1, g, 1)
                    dve.reciprocal(lrs[kk], lrt[kk]).then_inc(nn, 1)
                    need(dve, nn, 2, g, 1)
                    tt(slots(nd[kk]), slots(nd[kk]), per_slot(lrs[kk]), ALU.mult).then_inc(nn, 1)

                def qkv_out(p):
                    need(dve, qkv_ps, 4, i0, p + 1)
                    if p == 0:
                        need(dve, qk_norm, 1, i1, 1)
                        need(dve, squared, 1, i1, 1)
                        need(dve, pv_ps, 1, i4, 1)
                    tt(qk[:, 2 * p:2 * p + 2, :],
                       mmb[p % 2][:, 0:6 * C].rearrange("p (s n) -> p s n", s=2)[:, :, 0:2 * C],
                       bqk.unsqueeze(1).to_broadcast([P, 2, 2 * C]), ALU.add).then_inc(qkv_sb, 1)
                    dve.tensor_copy(vpad[k][:, 2 * p:2 * p + 2, :, 0:HD],
                                    mmb[p % 2][:, 0:6 * C].rearrange("p (s n) -> p s n", s=2)[:, :, 2 * C:3 * C]
                                    .rearrange("p s (h d) -> p s h d", h=HEADS)).then_inc(v_put, 1)

                if there(i3):
                    need(dve, proj_ps, 1, i3, 1)
                    norm_sum(acc, 0, ln1_d)
                if there(i0):
                    qkv_out(0)
                if there(i3):
                    need(dve, x1_sb, 3, i4, 2)
                    norm_nd(acc, i3, 0, ln1_d)
                if there(i0):
                    qkv_out(1)
                if there(i2):
                    need(dve, exped, 1, i2, 1)
                    dve.tensor_reduce(sm, pr3, AX.X, ALU.add).then_inc(prob_sum, 1)
                    need(dve, prob_sum, 2, i2, 1)
                    need(dve, probs, 1, i3, 1)
                    dve.reciprocal(rs, sm).then_inc(prob_sum, 1)
                if there(i0):
                    qkv_out(2)
                    qkv_out(3)
                if there(i3):
                    norm_var(i3, 0, ln1_sq, ln1_ss)
                if there(i6):
                    norm_var(i6, 1, ln2_sq, ln2_ss)
                if there(i0):
                    need(dve, squared, 1, i0, 1)
                    need(dve, rooted, 1, i1, 1)
                    dve.tensor_reduce(ss, sq.rearrange("p (n d) -> p n d", d=HD), AX.X, ALU.add).then_inc(summed, 1)
                    need(dve, summed, 2, i0, 1)
                    ts(ss, ss, 1e-24, None, ALU.max).then_inc(summed, 1)
                if there(i2):
                    need(dve, probs, 1, i2, 1)
                    need(dve, pv_ps, 1, i3, 1)
                    dve.transpose(probT.rearrange("p h s n -> p (h s n)"),
                                  prob.rearrange("p h s m -> p (h s m)")).then_inc(probT_sb, 1)
                if there(i1):
                    need(dve, S_ps, 1, i1, 1)
                    need(dve, probT_sb, 1, i2, 1)
                    tt(prob, S, relb.unsqueeze(2).to_broadcast([P, HEADS, SLOTS, 32]), ALU.add).then_inc(biased, 1)
                if there(i6):
                    norm_scale(i6, 1, ln2_rt, ln2_n)
                if there(i0):
                    need(dve, rooted, 1, i0, 1)
                    need(dve, qk_norm, 1, i1, 1)
                    dve.reciprocal(rn, rt).then_inc(factor, 1)
                    need(dve, factor, 2, i0, 1)
                    rq = rn.rearrange("p (s k h) -> p s k h", s=SLOTS, k=2)[:, :, 0, :]
                    tt(rq, rq, scale.unsqueeze(1).to_broadcast([P, SLOTS, HEADS]), ALU.mult).then_inc(factor, 1)
                if there(i3):
                    norm_scale(i3, 0, ln1_rt, ln1_n)
                if there(i1):
                    need(dve, biased, 1, i1, 1)
                    need(dve, shifted, 1, i2, 1)
                    dve.tensor_reduce(mx, pr3, AX.X, ALU.max).then_inc(maxed, 1)
                if there(i5):
                    need(dve, h_ps, 1, i5, 1)
                    norm_sum(acc, 1, ln2_d)
                    need(dve, y_sb, 2, i6, 2)
                    norm_nd(acc, i5, 1, ln2_d)
                if there(i6):
                    need(dve, yT_ps, 1, i6, 1)
                    if k == 2 and not (isinstance(s, int) and s < 2):
                        dve.wait_ge(y_out, s * 32 - 32)
                    dve.tensor_copy(ystripe[:, :, (k - LAG) % GPS, :].rearrange("p r (i j) -> p i r j", j=CPS),
                                    tr.rearrange("p (i r j) -> p i r j", i=PAIRS, j=CPS)).then_inc(yT_sb, 1)

            over_groups(dve, step)

            def put(b, cq, j):
                dve.wait_ge(o_ps, cq * NB + (b * NCH + j + 1))
                dve.tensor_copy(orow[:, :, :, bass.ds(cq * NB + j, 1)].rearrange("p k n c -> p (k n) c"),
                                ps[:, j, :].unsqueeze(2)).then_inc(o_dve, 1)

            dve.wait_ge(y_out, 32 * NS)
            for b in range(BL1):
                if b:
                    dve.wait_ge(rows_out, 64 * b)
                with dve.Fori(0, NCH // NB) as cq:
                    for j in (1, 3):
                        put(b, cq, j)

        @block.gpsimd
        def _(pool):
            tt = pool.tensor_tensor
            pool.memset(ident, 0.0).then_inc(made_id, 1)
            pool.wait_ge(made_id, 1)
            pool.affine_select(out=ident, in_=ident, compare_op=ALU.not_equal, fill=1.0, base=0,
                               pattern=[[-1, P]], channel_multiplier=1).then_inc(made_id, 1)
            pool.memset(qkn, 0.0).then_inc(made_id, 1)
            for v in vpad:
                pool.memset(v, 0.0).then_inc(made_id, 1)
            pool.wait_ge(made_id, 7)
            for v in vpad:
                pool.memset(v[:, :, :, HD:HD + 1], 1.0).then_inc(made_id, 1)
            pool.wait_ge(made_id, 11)
            pool.wait_ge(consts, consts_in)
            pool.tensor_copy(pickb, ident).then_inc(pick_made, 1)
            pool.wait_ge(pick_made, 1)
            tt(pickb[:, HD:HD + 1], pickb[:, HD:HD + 1], bvcol, ALU.add).then_inc(made_id, 1)

            def step(s, k):
                i0, i1, i2, i3, i4, i5, i6, i7 = (Group(s, k - d) for d in range(8))
                par = k % 2
                hs = HEADS * SLOTS
                pr3 = prob.rearrange("p h s m -> p (h s) m")
                if there(i2):
                    need(pool, prob_sum, 2, i2, 2)
                    tt(pr3, pr3, rs.unsqueeze(2).to_broadcast([P, hs, 32]), ALU.mult).then_inc(probs, 1)
                if there(i6):
                    need(pool, ln2_n, 2, i6, 2)
                    need(pool, yT_ps, 1, i7, 1)
                    tt(slots(nd[1]), slots(nd[1]), row(g2), ALU.mult).then_inc(y_sb, 1)
                    need(pool, y_sb, 2, i6, 1)
                    tt(yo, x1o2[(k - 6) % 4], nd[1], ALU.subtract).then_inc(y_sb, 1)
                if there(i0):
                    need(pool, factor, 2, i0, 2)
                    need(pool, qkT_ps, 4, i1, 4)
                    tt(qkn.rearrange("p s k h d -> p (s k h) d")[:, :, 0:HD],
                       qk.rearrange("p s (n d) -> p (s n) d", d=HD),
                       rn.unsqueeze(2).to_broadcast([P, SLOTS * 2 * HEADS, HD]), ALU.mult).then_inc(qk_norm, 1)
                if there(i3):
                    need(pool, ln1_n, 2, i3, 2)
                    need(pool, x1T_ps, 1, i5, 1)
                    tt(slots(nd[0]), slots(nd[0]), row(g1), ALU.mult).then_inc(x1_sb, 1)
                    need(pool, x1_sb, 3, i3, 1)
                    tt(x1[(k - 3) % 2], xo1[(k - 3) % 4], nd[0], ALU.subtract).then_inc(x1_sb, 1)
                if there(i1):
                    need(pool, maxed, 1, i1, 1)
                    tt(pr3, pr3, mx.unsqueeze(2).to_broadcast([P, hs, 32]), ALU.subtract).then_inc(shifted, 1)
                if there(i3):
                    need(pool, x1_sb, 3, i3, 2)
                    need(pool, y_sb, 2, i7, 2)
                    tt(slots(x1o2[(k - 3) % 4]), slots(x1[(k - 3) % 2]), row(o2), ALU.add).then_inc(x1_sb, 1)
                if there(i0):
                    pool.wait_ge(x_in[par], s * (2 * SLOTS * 16) + (k // 2 + 1) * SLOTS * 16)
                    tt(slots(xo1[k]), xin[par], row(o1), ALU.add).then_inc(xo_put, 1)

            over_groups(pool, step)


def arrays_of(inputs):
    L0, L1 = "L0_conv_", "L1_conv_"
    t = lambda n: np.ascontiguousarray(np.asarray(inputs[L0 + n]).T)
    row = lambda n: np.asarray(inputs[L0 + n]).reshape(1, -1)
    cols = lambda n: np.ascontiguousarray(np.asarray(inputs[L0 + n]).reshape(-1, P).T)
    a = {"x": np.asarray(inputs["x"]), "qkv_wt": t("qkv_w"), "qkv_b": row("qkv_b"),
         "v_b": np.asarray(inputs[L0 + "qkv_b"])[2 * C:].reshape(-1, 1), "proj_wt": t("proj_w"),
         "proj_b": row("proj_b"), "logit_scale": np.asarray(inputs[L0 + "logit_scale"]).reshape(-1),
         "cpb_w1t": t("cpb_w1"), "cpb_b1": cols("cpb_b1"), "cpb_w2t": t("cpb_w2"),
         "n1g": row("norm1_g"), "n1b": row("norm1_b"), "n2g": row("norm2_g"), "n2b": row("norm2_b"),
         "fc1_wt": t("fc1_w"), "fc1_b": cols("fc1_b"), "fc2_wt": t("fc2_w"), "fc2_b": np.asarray(inputs[L0 + "fc2_b"]).reshape(-1, 1),
         "w_real": np.asarray(inputs[L1 + "w_real"]), "w_imag": np.asarray(inputs[L1 + "w_imag"])}
    a.update(shape_constants())
    return a


def kernel(**inputs):
    import concourse.bacc as _bacc
    from concourse.bass_utils import run_bass_kernel_spmd as _run

    nc = _bacc.Bacc("TRN2", target_bir_lowering=False, num_devices=1)
    arrays, args = {}, []
    for name, a in arrays_of(inputs).items():
        arrays[f"in_{name}"] = a
        args.append(nc.dram_tensor(f"in_{name}", a.shape, F32, kind="ExternalInput").ap())
    shape = tuple(inputs["x"].shape)
    args.append(nc.dram_tensor("out", shape, F32, kind="ExternalOutput").ap())
    b, h, w, c = shape
    args.append(nc.dram_tensor("y", (b, h, c, w), F32, kind="Internal").ap())
    args.append(nc.dram_tensor("mix", (C, P, 2 * T), F32, kind="Internal").ap())
    swin_then_fourier(nc, *args)
    r = _run(nc, [arrays], core_ids=[0])
    return r.results[0]["out"]
```
